# Optimizing a Trainium2 kernel written in Bass

```python
import numpy as np
import jax
import jax.numpy as jnp

def _softmax(x, axis=-1):
    return jax.nn.softmax(x, axis=axis)

def _gelu(x):
    return jax.nn.gelu(x, approximate=True)

def _silu(x):
    return jax.nn.silu(x)

def _sigmoid(x):
    return jax.nn.sigmoid(x)

def _layernorm(x, axis=-1, eps=1e-05):
    m = jnp.mean(x, axis=axis, keepdims=True)
    v = jnp.var(x, axis=axis, keepdims=True)
    return (x - m) / jnp.sqrt(v + eps)

def _scatter_add(tgt, idx, src, axis=0):
    return tgt.at[idx].add(src)

def _segment_sum(src, seg, n):
    return jax.ops.segment_sum(src, seg, n)
kernel_name = 'mk_xattn_ffn_d1_seqx_r4_7472c3'

def setup_inputs(seed: int=0):
    np.random.seed(seed)
    _w = jnp.asarray

    def _rec_inputs():
        import jax
        import jax.numpy as jnp
        _rk = jax.random.key(seed)
        x = -0.0003929 + 0.9999 * jax.random.normal(jax.random.fold_in(_rk, 1), (64, 128, 512), jnp.float32)
        _lenS = 128 - jax.random.randint(jax.random.fold_in(_rk, 7), (64,), 0, max(1, 128 // 4) + 1, jnp.int32)
        _lenS2 = 128 - jax.random.randint(jax.random.fold_in(_rk, 8), (64,), 0, max(1, 128 // 4) + 1, jnp.int32)
        _ctx_2048P = jax.random.normal(jax.random.fold_in(_rk, 11), (64, 16, 512), jnp.float32)
        _ctx_2048c = jax.random.dirichlet(jax.random.fold_in(_rk, 511), 0.3 * jnp.ones((16,), jnp.float32), (64, 128))
        _ctx_2048t = jnp.einsum('bsk,bkd->bsd', _ctx_2048c, _ctx_2048P)
        _ctx_2048t = _ctx_2048t * jax.lax.rsqrt(jnp.mean(jnp.square(_ctx_2048t)) + 1e-12) * 0.953939
        ctx_2048 = 4.13588e-05 + 0.999923 * (_ctx_2048t + 0.3 * jax.random.normal(jax.random.fold_in(_rk, 611), (64, 128, 512), jnp.float32))
        return (x, ctx_2048)
    x, ctx_2048 = _rec_inputs()

    def _L0_xattn_setup():
        import jax, jax.numpy as jnp
        import numpy as np
        HIDDEN = 512
        N_HEADS = 16
        N_KV_HEADS = 4
        HEAD_DIM = 128
        EPS = 1e-06

        def rms_norm(x, w, eps=EPS):
            xf = x.astype(jnp.float32)
            var = jnp.mean(xf * xf, axis=-1, keepdims=True)
            return w * (xf * jax.lax.rsqrt(var + eps)).astype(x.dtype)
        key = jax.random.key(seed)
        ks = jax.random.split(key, 8)
        B, S, S_ENC = (4, 512, 256)
        inner = N_HEADS * HEAD_DIM
        kv_dim = N_KV_HEADS * HEAD_DIM
        s = 0.02
        return {'hidden_states': jax.random.normal(ks[0], (B, S, HIDDEN), jnp.float32), 'encoder_hidden_states': jax.random.normal(ks[1], (B, S_ENC, HIDDEN), jnp.float32), 'Wq': jax.random.normal(ks[2], (HIDDEN, inner), jnp.float32) * s, 'Wk': jax.random.normal(ks[3], (HIDDEN, kv_dim), jnp.float32) * s, 'Wv': jax.random.normal(ks[4], (HIDDEN, kv_dim), jnp.float32) * s, 'Wo': jax.random.normal(ks[5], (inner, HIDDEN), jnp.float32) * s, 'q_norm_w': jnp.ones((HEAD_DIM,), jnp.float32), 'k_norm_w': jnp.ones((HEAD_DIM,), jnp.float32)}
    _L0_xattn_all = _L0_xattn_setup()
    _L0_xattn_in = {k: v for k, v in _L0_xattn_all.items() if k in ('Wq', 'Wk', 'Wv', 'Wo', 'q_norm_w', 'k_norm_w')}
    del _L0_xattn_all

    def _L0_ffn_setup():
        import jax, jax.numpy as jnp
        import numpy as np
        import math
        NUM_EXPERTS = 12
        TOP_K = 2
        CAP_FACTOR = 1.25
        key = jax.random.key(seed)
        k0, k1, k2, k3, k4 = jax.random.split(key, 5)
        B, S, H, F = (4, 1024, 512, 64)
        hidden_states = jax.random.normal(k0, (B, S, H), jnp.float32)
        gate_w = jax.random.normal(k1, (NUM_EXPERTS, H), jnp.float32) * 0.02
        w1 = jax.random.normal(k2, (NUM_EXPERTS, F, H), jnp.float32) * 0.02
        w2 = jax.random.normal(k3, (NUM_EXPERTS, H, F), jnp.float32) * 0.02
        w3 = jax.random.normal(k4, (NUM_EXPERTS, F, H), jnp.float32) * 0.02
        return dict(hidden_states=hidden_states, gate_w=gate_w, w1=w1, w2=w2, w3=w3)
    _L0_ffn_all = _L0_ffn_setup()
    _L0_ffn_in = {k: v for k, v in _L0_ffn_all.items() if k in ('gate_w', 'w1', 'w2', 'w3')}
    del _L0_ffn_all
    return {'x': x, 'ctx_2048': ctx_2048, 'L0_xattn_Wq': _L0_xattn_in['Wq'], 'L0_xattn_Wk': _L0_xattn_in['Wk'], 'L0_xattn_Wv': _L0_xattn_in['Wv'], 'L0_xattn_Wo': _L0_xattn_in['Wo'], 'L0_xattn_q_norm_w': _L0_xattn_in['q_norm_w'], 'L0_xattn_k_norm_w': _L0_xattn_in['k_norm_w'], 'L0_ffn_gate_w': _L0_ffn_in['gate_w'], 'L0_ffn_w1': _L0_ffn_in['w1'], 'L0_ffn_w2': _L0_ffn_in['w2'], 'L0_ffn_w3': _L0_ffn_in['w3']}

def reference(x, ctx_2048, L0_xattn_Wq, L0_xattn_Wk, L0_xattn_Wv, L0_xattn_Wo, L0_xattn_q_norm_w, L0_xattn_k_norm_w, L0_ffn_gate_w, L0_ffn_w1, L0_ffn_w2, L0_ffn_w3):
    import jax
    import jax.numpy as jnp

    def _L0_xattn_ref(hidden_states, encoder_hidden_states, Wq, Wk, Wv, Wo, q_norm_w, k_norm_w):
        import jax, jax.numpy as jnp
        import numpy as np
        HIDDEN = 512
        N_HEADS = 16
        N_KV_HEADS = 4
        HEAD_DIM = 128
        EPS = 1e-06

        def rms_norm(x, w, eps=EPS):
            xf = x.astype(jnp.float32)
            var = jnp.mean(xf * xf, axis=-1, keepdims=True)
            return w * (xf * jax.lax.rsqrt(var + eps)).astype(x.dtype)
        B, S, _ = hidden_states.shape
        S_enc = encoder_hidden_states.shape[1]
        groups = N_HEADS // N_KV_HEADS
        scale = 1.0 / HEAD_DIM ** 0.5
        q = (hidden_states @ Wq).reshape(B, S, N_HEADS, HEAD_DIM)
        k = (encoder_hidden_states @ Wk).reshape(B, S_enc, N_KV_HEADS, HEAD_DIM)
        v = (encoder_hidden_states @ Wv).reshape(B, S_enc, N_KV_HEADS, HEAD_DIM)
        q = rms_norm(q, q_norm_w)
        k = rms_norm(k, k_norm_w)
        k = jnp.repeat(k, groups, axis=2)
        v = jnp.repeat(v, groups, axis=2)
        scores = jnp.einsum('bqhd,bkhd->bhqk', q, k) * scale
        probs = jax.nn.softmax(scores, axis=-1)
        out = jnp.einsum('bhqk,bkhd->bqhd', probs, v)
        out = out.reshape(B, S, N_HEADS * HEAD_DIM)
        return out @ Wo

    def _L0_ffn_ref(hidden_states, gate_w, w1, w2, w3):
        import jax, jax.numpy as jnp
        import numpy as np
        import math
        NUM_EXPERTS = 12
        TOP_K = 2
        CAP_FACTOR = 1.25
        B, S, H = hidden_states.shape
        T = B * S
        E = gate_w.shape[0]
        cap = math.ceil(T / E * CAP_FACTOR)
        x = hidden_states.reshape(T, H)
        logits = x @ gate_w.T
        probs = jax.nn.softmax(logits, axis=-1)
        rw, sel = jax.lax.top_k(probs, TOP_K)
        rw = rw / rw.sum(axis=-1, keepdims=True)
        ar_cap = jnp.arange(cap)
        ar_flat = jnp.arange(TOP_K * T, dtype=jnp.int32)

        def per_expert(e, we1, we2, we3):
            mask = sel.T == e
            fm = mask.ravel()
            pos = jnp.cumsum(fm) - 1
            slot_idx = jnp.where(fm & (pos < cap), pos, cap)
            buf = jnp.zeros(cap + 1, jnp.int32).at[slot_idx].set(ar_flat)
            flat = buf[:cap]
            valid = ar_cap < fm.sum()
            tok = flat % T
            slot = flat // T
            xs = x[tok]
            h = jax.nn.silu(xs @ we1.T * (xs @ we3.T)) @ we2.T
            w = jnp.where(valid, rw[tok, slot], 0.0)
            return (tok, h * w[:, None])
        toks, contribs = jax.vmap(per_expert)(jnp.arange(E), w1, w2, w3)
        out = jnp.zeros((T, H), x.dtype).at[toks.ravel()].add(contribs.reshape(-1, H))
        return out.reshape(B, S, H)
    x = x + _L0_xattn_ref(_layernorm(x, axis=-1), ctx_2048, L0_xattn_Wq, L0_xattn_Wk, L0_xattn_Wv, L0_xattn_Wo, L0_xattn_q_norm_w, L0_xattn_k_norm_w)
    x = x + _L0_ffn_ref(_layernorm(x, axis=-1), L0_ffn_gate_w, L0_ffn_w1, L0_ffn_w2, L0_ffn_w3)
    return x

_drawn_inputs = setup_inputs


def setup_inputs(seed=0):
    import zlib

    import numpy as np

    out = dict(_drawn_inputs(seed))
    spreads = {'L0_xattn_q_norm_w': (1.0, 0.6), 'L0_xattn_k_norm_w': (1.0, 0.6)}
    factors = {'L0_ffn_gate_w': 6.026, 'L0_ffn_w1': 5.738, 'L0_ffn_w2': 5.652, 'L0_ffn_w3': 5.732}
    for name, (base, spread) in spreads.items():
        noise = np.random.default_rng([zlib.crc32(name.encode()), seed]).standard_normal(out[name].shape)
        drawn = base * np.exp(spread * noise) if base else spread * noise
        out[name] = jnp.asarray(drawn.astype(out[name].dtype))
    for name, factor in factors.items():
        out[name] = (out[name] * factor).astype(out[name].dtype)
    return out
```

```python
from contextlib import ExitStack

import numpy as np

import concourse.bass as bass
from concourse import mybir
from concourse.alu_op_type import AluOpType as ALU

NB, SEQ, HID = 64, 128, 512
NH, NG, HD = 16, 4, 128
HPG = NH // NG
NC = HID // 128
NU = NB * NG
T = NB * SEQ
E, F = 12, 64
CAP = -(-T * 5 // (4 * E))
NT = -(-CAP // 128)
CP = NT * 128
STRIDE = 2 * CP
BIG = 1 << 20
TABW = 6
ATTN_EPS, LN_EPS = 1e-6, 1e-5


def experts(nc, gt, w13, w2T, out):
    f32, i32 = mybir.dt.float32, mybir.dt.int32
    ACT = mybir.ActivationFunctionType
    AX = mybir.AxisListType
    wait, sem, pb, ident, ones_b, tab, iota12, macc = (gt[k] for k in (
        "wait", "sem", "pb", "ident", "ones_b", "tab", "iota12", "macc"))
    wait_apart = gt["wait_apart"]
    x1_d, xn2_d, table_d, y_d, LIST1 = (gt[k] for k in ("x1_d", "xn2_d", "table_d", "y_d", "LIST1"))

    with ExitStack() as ctx:
        def sb(name, shape, dt=f32):
            return ctx.enter_context(nc.sbuf_tensor(name, shape, dt))

        rows = sb("rows", [128, NB, 2], i32)
        wts = sb("wts", [128, NB, 2])
        zero = sb("zero", [128, 1])

        with ExitStack() as c2:
            def sb2(name, shape, dt=f32):
                return c2.enter_context(nc.sbuf_tensor(name, shape, dt))

            tot = sb2("tot", [128, 2 * E])
            first_n = sb2("first_n", [128, E], i32)
            n_f = sb2("n_f", [128, E])
            one_hot = sb2("one_hot", [128, NB, E])
            base = sb2("base", [128, NB])
            pos = sb2("pos", [128, NB, 2])
            over = sb2("over_all", [128, NB, 2])
            rowf = sb2("rowf", [128, NB, 2])
            e10 = sb2("e10", [128, NB])
            den = sb2("den", [128, NB])
            kept = sb2("kept", [128, NB, 2])
            tv = tab[:, :].rearrange("p (b w) -> p b w", w=TABW)
            s_tot, s_n, d_tab, s_e = sem("totals_done"), sem("first_n_done"), sem("d_tables_joined"), sem("e10_done")
            ch = sem("dve_chain")
            block = c2.enter_context(nc.Block())

            @block.tensor
            def _(pe):
                nc.tensor.matmul(pb[0][:, 0:2 * E], ones_b[:, :], macc[:, :], start=True, stop=True).then_inc(s_tot, 1)

            @block.scalar
            def _(act):
                nc.scalar.activation(e10[:, :], tv[:, :, 4], ACT.Exp).then_inc(s_e, 1)

            @block.sync
            def _(sp):
                sp.wait_ge(s_n, 1)
                for e in range(E):
                    n = sp.value_load(first_n[0:1, e:e + 1], min_val=0, max_val=CAP)
                    sp.dma_start(table_d[bass.ds(n + e * STRIDE, CP), :],
                                 table_d[LIST1 + e * CP:LIST1 + (e + 1) * CP, :]).then_inc(d_tab, 16)
                sp.wait_ge(d_tab, 16 * E)

            @block.vector
            def _(dve):
                n = [0]

                def then(ins):
                    n[0] += 1
                    ins.then_inc(ch, 1)
                    dve.wait_ge(ch, n[0])

                nc.vector.memset(zero[:, :], 0.0)
                dve.wait_ge(s_tot, 1)
                then(nc.vector.tensor_copy(tot[:, :], pb[0][:, 0:2 * E]))
                then(nc.vector.tensor_scalar(n_f[:, :], tot[:, 0:E], float(CAP), None, ALU.min))
                nc.vector.tensor_copy(first_n[:, :], n_f[:, :]).then_inc(s_n, 1)
                then(nc.vector.tensor_tensor(one_hot[:, :, :], iota12[:, None, :].broadcast_to([128, NB, E]),
                                             tv[:, :, 1:2].broadcast_to([128, NB, E]), ALU.is_equal))
                then(nc.vector.tensor_tensor(one_hot[:, :, :], one_hot[:, :, :],
                                             tot[:, None, 0:E].broadcast_to([128, NB, E]), ALU.mult))
                then(nc.vector.tensor_reduce(base[:, :], one_hot[:, :, :], AX.X, ALU.add))
                nc.vector.tensor_copy(pos[:, :, 0], tv[:, :, 2])
                then(nc.vector.tensor_tensor(pos[:, :, 1], base[:, :], tv[:, :, 3], ALU.add))
                nc.vector.tensor_scalar(kept[:, :, :], pos[:, :, :], float(CAP), None, ALU.is_lt)
                then(nc.vector.tensor_scalar(over[:, :, :], pos[:, :, :], float(CAP), float(BIG), ALU.is_ge, ALU.mult))
                then(nc.vector.tensor_tensor(over[:, :, :], over[:, :, :], pos[:, :, :], ALU.add))
                then(nc.vector.scalar_tensor_tensor(out=rowf[:, :, :], in0=tv[:, :, 0:2], scalar=float(CP),
                                                    in1=over[:, :, :], op0=ALU.mult, op1=ALU.add))
                nc.vector.tensor_copy(rows[:, :, :], rowf[:, :, :])
                dve.wait_ge(s_e, 1)
                then(nc.vector.tensor_scalar(den[:, :], e10[:, :], 1.0, None, ALU.add))
                then(nc.vector.reciprocal(den[:, :], den[:, :]))
                nc.vector.tensor_tensor(wts[:, :, 0], den[:, :], kept[:, :, 0], ALU.mult)
                then(nc.vector.tensor_tensor(den[:, :], den[:, :], e10[:, :], ALU.mult))
                then(nc.vector.tensor_tensor(wts[:, :, 1], den[:, :], kept[:, :, 1], ALU.mult))

        with ExitStack() as c3:
            def sb3(name, shape, dt=f32):
                return c3.enter_context(nc.sbuf_tensor(name, shape, dt))

            w13_s = [sb3(f"w13_{i}", [128, NC, 2 * F]) for i in range(2)]
            w2_s = [sb3(f"w2_{i}", [F, HID]) for i in range(2)]
            idx = [sb3(f"idx_{i}", [128, NT], i32) for i in range(2)]
            xg = [sb3(f"xg_{i}", [128, NT, HID]) for i in range(2)]
            xgT = sb3("xgT", [128, NC, CP])
            h3, g13, eg, hT = (sb3(nm, [F, CP]) for nm in ("h3", "g13", "eg", "hT"))
            yb = [sb3(f"yb_{i}", [128, NT, HID]) for i in range(2)]
            d_w = [sem(f"d_expert_w{i}") for i in range(2)]
            d_i = [sem(f"d_idx{i}") for i in range(2)]
            d_g = [sem(f"d_gathered{i}") for i in range(2)]
            d_y = [sem(f"d_y_stored{i}") for i in range(2)]
            w_used = [sem(f"expert_w_used{i}") for i in range(2)]
            xg_used = [sem(f"xg_used{i}") for i in range(2)]
            s_z = sem("xg_zeroed")
            tr_done = [sem("xg_tr_even"), sem("xg_tr_odd")]
            ev_done = [sem("xgT_even"), sem("xgT_odd")]
            y_done = [sem("y_even"), sem("y_odd")]
            yev_done = [sem("yb_even"), sem("yb_odd")]
            h_done, h3_done, g_done, e_done, dn_done, rc_done, hs_done, hT_used = (sem(nm) for nm in (
                "h_done", "h3_copied", "g13_done", "exp_g_done", "den_done", "recip_done", "h_silu_done", "hT_used"))
            block = c3.enter_context(nc.Block())
            HALF = [(0, 512), (512, CP)]
            CNT = [(NT + 1) // 2, NT // 2]
            PAIRS = E // 2

            @block.sync
            def _(sp):
                def load(j, i):
                    e = 2 * j + i
                    wait(sp, w_used[i], j)
                    sp.dma_start(w13_s[i][:, :, :], w13[e]).then_inc(d_w[i], 16)
                    sp.dma_start(w2_s[i][:, :], w2T[e]).then_inc(d_w[i], 16)
                    wait_apart(sp, (d_g[i], 16 * NT * j))
                    sp.dma_start(idx[i][:, :], table_d[bass.ds(e * STRIDE, CP), :].rearrange(
                        "(p t) o -> p (t o)", t=NT)).then_inc(d_i[i], 16)

                def store(j, i):
                    e = 2 * j + i
                    wait_apart(sp, *[(yev_done[p], CNT[p] * (e + 1)) for p in range(2)])
                    sp.dma_start(y_d[bass.ds(e * CP, CP), :].rearrange("(p t) n -> p (t n)", t=NT),
                                 yb[i][:, :, :].rearrange("p t n -> p (t n)")).then_inc(d_y[i], 16)

                load(0, 0)
                load(0, 1)
                for i in range(2):
                    store(0, i)
                    load(1, i)
                with sp.Fori(1, PAIRS - 1) as j:
                    for i in range(2):
                        store(j, i)
                        load(j + 1, i)
                for i in range(2):
                    store(PAIRS - 1, i)
                for i in range(2):
                    sp.wait_ge(d_y[i], 16 * PAIRS)

            @block.gpsimd
            def _(pool):
                for i in range(2):
                    nc.gpsimd.memset(xg[i][:, :, :], 0.0).then_inc(s_z, 1)
                pool.wait_ge(s_z, 2)

                def gather(j, i):
                    wait_apart(pool, (d_i[i], 16 * j + 16), (xg_used[i], j))
                    for t in range(NT):
                        nc.gpsimd.indirect_dma_start(
                            out=xg[i][:, t, :], out_offset=None, in_=xn2_d,
                            in_offset=bass.IndirectOffsetOnAxis(ap=idx[i][:, t:t + 1], axis=0),
                            bounds_check=T - 1, oob_is_err=False).then_inc(d_g[i], 16)

                gather(0, 0)
                gather(0, 1)
                with pool.Fori(1, PAIRS) as j:
                    gather(j, 0)
                    gather(j, 1)

            @block.tensor
            def _(pe):
                def transposes(j, i):
                    e = 2 * j + i
                    pe.wait_ge(d_g[i], 16 * NT * (j + 1))
                    for t in range(NT):
                        p = t % 2
                        wait(pe, ev_done[p], CNT[p] * e + t // 2)
                        for c in range(NC):
                            tr = nc.tensor.transpose(pb[p][:, c * 128:(c + 1) * 128],
                                                     xg[i][:, t, c * 128:(c + 1) * 128], ident[:, :])
                        tr.then_inc(tr_done[p], 1)
                    pe.wait_ge(tr_done[(NT - 1) % 2], CNT[(NT - 1) % 2] * (e + 1))
                    pe.sem_inc(xg_used[i], 1)

                def up(j, i):
                    e = 2 * j + i
                    pe.wait_ge(d_w[i], 32 * (j + 1))
                    for p in range(2):
                        pe.wait_ge(ev_done[p], CNT[p] * (e + 1))
                    for k, (lo, hi) in enumerate(HALF):
                        wait(pe, g_done, 2 * e)
                        for c in range(NC):
                            mm = nc.tensor.matmul(pb[2 + k][:, 0:hi - lo], w13_s[i][:, c, :], xgT[:, c, lo:hi],
                                                  start=(c == 0), stop=(c == NC - 1))
                        mm.then_inc(h_done, 1)

                def down(j, i):
                    e = 2 * j + i
                    pe.wait_ge(hs_done, e + 1)
                    for t in range(NT):
                        p = t % 2
                        wait(pe, yev_done[p], CNT[p] * e + max(0, t // 2 - 1))
                        nc.tensor.matmul(pb[4 + t % 4][:, :], hT[:, t * 128:(t + 1) * 128], w2_s[i][:, :],
                                         start=True, stop=True).then_inc(y_done[p], 1)
                    pe.wait_ge(y_done[(NT - 1) % 2], CNT[(NT - 1) % 2] * (e + 1))
                    pe.sem_inc(w_used[i], 1)
                    pe.sem_inc(hT_used, 1)

                def step(j, i, more=True):
                    up(j, i)
                    if more:
                        transposes(j + i, 1 - i)
                    down(j, i)

                transposes(0, 0)
                step(0, 0)
                step(0, 1)
                with pe.Fori(1, PAIRS - 1) as j:
                    step(j, 0)
                    step(j, 1)
                step(PAIRS - 1, 0)
                step(PAIRS - 1, 1, more=False)

            def copy_tiles(eng, copy, p, j, i):
                e = 2 * j + i
                wait(eng, h_done, 2 * e)
                for n, t in enumerate(range(p, NT, 2)):
                    eng.wait_ge(tr_done[p], CNT[p] * e + n + 1)
                    copy(xgT[:, :, t * 128:(t + 1) * 128],
                         pb[p][:, :].rearrange("p (c t) -> p c t", c=NC)).then_inc(ev_done[p], 1)

            def copy_outputs(eng, copy, p, j, i):
                e = 2 * j + i
                wait(eng, d_y[i], 16 * j)
                for n, t in enumerate(range(p, NT, 2)):
                    eng.wait_ge(y_done[p], CNT[p] * e + n + 1)
                    copy(yb[i][:, t, :], pb[4 + t % 4][:, :]).then_inc(yev_done[p], 1)

            @block.scalar
            def _(act):
                def step(j, i, more=True):
                    e = 2 * j + i
                    wait(act, g_done, 2 * e)
                    for k, (lo, hi) in enumerate(HALF):
                        act.wait_ge(h_done, 2 * e + k + 1)
                        nc.scalar.copy(h3[:, lo:hi], pb[2 + k][F:2 * F, 0:hi - lo]).then_inc(h3_done, 1)
                    act.wait_ge(g_done, 2 * e + 2)
                    wait(act, hs_done, e)
                    nc.scalar.activation(eg[:, :], g13[:, :], ACT.Exp, scale=-1.0).then_inc(e_done, 1)
                    if more:
                        copy_tiles(act, nc.scalar.copy, 0, j + i, 1 - i)
                    copy_outputs(act, nc.scalar.copy, 0, j, i)

                copy_tiles(act, nc.scalar.copy, 0, 0, 0)
                step(0, 0)
                step(0, 1)
                with act.Fori(1, PAIRS - 1) as j:
                    step(j, 0)
                    step(j, 1)
                step(PAIRS - 1, 0)
                step(PAIRS - 1, 1, more=False)

            @block.vector
            def _(dve):
                def step(j, i, more=True):
                    e = 2 * j + i
                    for k, (lo, hi) in enumerate(HALF):
                        dve.wait_ge(h3_done, 2 * e + k + 1)
                        nc.vector.tensor_tensor(g13[:, lo:hi], pb[2 + k][0:F, 0:hi - lo], h3[:, lo:hi],
                                                ALU.mult).then_inc(g_done, 1)
                    dve.wait_ge(e_done, e + 1)
                    nc.vector.tensor_scalar(eg[:, :], eg[:, :], 1.0, None, ALU.add).then_inc(dn_done, 1)
                    dve.wait_ge(dn_done, e + 1)
                    nc.vector.reciprocal(eg[:, :], eg[:, :]).then_inc(rc_done, 1)
                    dve.wait_ge(rc_done, e + 1)
                    wait(dve, hT_used, e)
                    nc.vector.tensor_tensor(hT[:, :], g13[:, :], eg[:, :], ALU.mult).then_inc(hs_done, 1)
                    if more:
                        copy_tiles(dve, nc.vector.tensor_copy, 1, j + i, 1 - i)
                    copy_outputs(dve, nc.vector.tensor_copy, 1, j, i)

                copy_tiles(dve, nc.vector.tensor_copy, 1, 0, 0)
                step(0, 0)
                step(0, 1)
                with dve.Fori(1, PAIRS - 1) as j:
                    step(j, 0)
                    step(j, 1)
                step(PAIRS - 1, 0)
                step(PAIRS - 1, 1, more=False)

        with ExitStack() as c4:
            R = 4
            yr = [[c4.enter_context(nc.sbuf_tensor(f"yr{k}_{i}", [128, HID], f32)) for k in range(2)] for i in range(R)]
            xo = [c4.enter_context(nc.sbuf_tensor(f"xo_{i}", [128, HID], f32)) for i in range(R)]
            rc = [c4.enter_context(nc.sbuf_tensor(f"row_{i}", [128, 2], i32)) for i in range(R)]
            wc = [c4.enter_context(nc.sbuf_tensor(f"wt_{i}", [128, 2], f32)) for i in range(R)]
            d_x = [sem(f"d_x1_back{i}") for i in range(R)]
            d_r = [sem(f"d_rows{i}") for i in range(R)]
            d_o = [sem(f"d_out{i}") for i in range(R)]
            s_z, s_rc, s_wc, s_a, s_b = (sem(nm) for nm in (
                "rows_zeroed", "row_numbers", "row_weights", "sum_first", "sum_both"))
            block = c4.enter_context(nc.Block())

            @block.scalar
            def _(act):
                def load(j):
                    for i in range(R):
                        wait(act, d_o[i], 16 * j)
                        act.dma_start(xo[i][:, :], x1_d[R * j + i]).then_inc(d_x[i], 16)

                load(0)
                with act.Fori(1, NB // R) as j:
                    load(j)

            @block.gpsimd
            def _(pool):
                for i in range(R):
                    for k in range(2):
                        nc.gpsimd.memset(yr[i][k][:, :], 0.0).then_inc(s_z, 1)
                pool.wait_ge(s_z, 2 * R)

                def gather(j):
                    for i in range(R):
                        b = R * j + i
                        wait(pool, d_r[i], 32 * j)
                        nc.gpsimd.tensor_copy(rc[i][:, :], rows[:, :, :].rearrange("p b k -> p (b k)")[
                            :, bass.ds(2 * b, 2)]).then_inc(s_rc, 1)
                        wait_apart(pool, (s_rc, b + 1), (s_b, R * j))
                        for k in range(2):
                            nc.gpsimd.indirect_dma_start(
                                out=yr[i][k][:, :], out_offset=None, in_=y_d,
                                in_offset=bass.IndirectOffsetOnAxis(ap=rc[i][:, k:k + 1], axis=0),
                                bounds_check=E * CP - 1, oob_is_err=False).then_inc(d_r[i], 16)

                gather(0)
                with pool.Fori(1, NB // R) as j:
                    gather(j)

            @block.vector
            def _(dve):
                with dve.Fori(0, NB // R) as j:
                    for i in range(R):
                        b = R * j + i
                        nc.vector.tensor_copy(wc[i][:, :], wts[:, :, :].rearrange("p b k -> p (b k)")[
                            :, bass.ds(2 * b, 2)]).then_inc(s_wc, 1)
                        dve.wait_ge(s_wc, b + 1)
                        dve.wait_ge(d_x[i], 16 * j + 16)
                        dve.wait_ge(d_r[i], 32 * j + 32)
                        nc.vector.scalar_tensor_tensor(out=xo[i][:, :], in0=yr[i][0][:, :], scalar=wc[i][:, 0:1],
                                                       in1=xo[i][:, :], op0=ALU.mult, op1=ALU.add).then_inc(s_a, 1)
                        dve.wait_ge(s_a, b + 1)
                        nc.vector.scalar_tensor_tensor(out=xo[i][:, :], in0=yr[i][1][:, :], scalar=wc[i][:, 1:2],
                                                       in1=xo[i][:, :], op0=ALU.mult, op1=ALU.add).then_inc(s_b, 1)

            @block.sync
            def _(sp):
                with sp.Fori(0, NB // R) as j:
                    for i in range(R):
                        wait(sp, s_b, R * j + i + 1)
                        sp.dma_start(out[R * j + i], xo[i][:, :]).then_inc(d_o[i], 16)
                for i in range(R):
                    sp.wait_ge(d_o[i], 16 * NB // R)



def build(nc, x, xT, cT, wq, wk, wv, wo, qw, kw, gateT, w13, w2T, out):
    f32, f32r, bf16, i32, u32 = (mybir.dt.float32, mybir.dt.float32r, mybir.dt.bfloat16,
                                 mybir.dt.int32, mybir.dt.uint32)
    ACT = mybir.ActivationFunctionType
    AX = mybir.AxisListType

    x1_d = nc.dram_tensor("x1_scratch", (NB, 128, HID), f32, kind="Internal").ap()
    xn2_d = nc.dram_tensor("xn2_scratch", (T, HID), f32, kind="Internal").ap()
    table_d = nc.dram_tensor("token_table", (E * STRIDE + E * CP, 1), i32, kind="Internal").ap()
    LIST1 = E * STRIDE
    y_d = nc.dram_tensor("expert_rows", (E * CP, HID), f32, kind="Internal").ap()

    def wait(eng, sem, n, apart=False):
        if isinstance(n, int) and n <= 0:
            return
        if apart:
            wait_apart(eng, (sem, n))
        else:
            eng.wait_ge(sem, n)

    def wait_apart(eng, *pairs):
        with ExitStack() as regs:
            values = []
            for s, n in pairs:
                if not isinstance(n, int):
                    reg = regs.enter_context(eng.register(f"wait_{s.name}_{nc.next_id()}"))
                    eng.reg_add(reg, n, 0)
                    n = reg
                values.append((s, n))
            eng.wait_ge(s_const, 1)
            for s, n in values:
                if not (isinstance(n, int) and n <= 0):
                    eng.wait_ge(s, n)

    keep = ExitStack()
    with keep:
        def sem(name):
            return keep.enter_context(nc.semaphore(name))

        def psum(name):
            return keep.enter_context(nc.psum_tensor(name, [128, 512], f32))

        ident = keep.enter_context(nc.sbuf_tensor("ident", [128, 128], f32))
        ones_b = keep.enter_context(nc.sbuf_tensor("ones_b", [128, 128], bf16))
        tab = keep.enter_context(nc.sbuf_tensor("tab", [128, NB * TABW], f32))
        iota12 = keep.enter_context(nc.sbuf_tensor("iota12", [128, E], f32))
        macc = keep.enter_context(nc.sbuf_tensor("macc", [128, 2 * E], bf16))
        pb = [psum(f"pb{i}") for i in range(8)]
        s_table, s_const = sem("s_table_scattered"), sem("s_const")

        with ExitStack() as ctx:
            def sb(name, shape, dt=f32):
                return ctx.enter_context(nc.sbuf_tensor(name, shape, dt))

            wqp = [sb(f"wq_{p}", [128, NC, NH * HD], f32r) for p in ("hi", "lo")]
            wkvp = [sb(f"wkv_{p}", [128, 2, NC, NG * HD], f32r) for p in ("hi", "lo")]
            wop = [sb(f"wo_{p}", [128, NH, HID], f32r) for p in ("hi", "lo")]
            xp = [sb(f"x_{p}", [128, NC, 128], f32r) for p in ("hi", "lo")]
            cp = [sb(f"c_{p}", [128, NC, 128], f32r) for p in ("hi", "lo")]
            qp = [sb(f"q_{p}", [128, HPG, 128], f32r) for p in ("hi", "lo")]
            kp = [sb(f"k_{p}", [128, NG, 128], f32r) for p in ("hi", "lo")]
            vp = [sb(f"v_{p}", [128, NG, HD], f32r) for p in ("hi", "lo")]
            ptp = [sb(f"pt_{p}", [128, HPG, 128], f32r) for p in ("hi", "lo")]
            otp = [sb(f"ot_{p}", [128, HPG, 128], f32r) for p in ("hi", "lo")]
            work = sb("work", [128, 8, 512])
            q_nat, probs, k_nat, xn2 = (work[:, i, :] for i in range(4))
            raw, x_stat, x_res = (work[:, i, :] for i in range(4, 7))
            junk = work[:, 7, :].rearrange("p (h t) -> p h t", h=4)
            xn2T = k_nat
            tri = sb("tri", [128, 128], bf16)
            gate = sb("gate", [128, NC, E])
            mean_w = tab[:, 0:128]
            sentinel = tab[:, 128:128 + E * CP // 128].bitcast(i32)

            small = sb("small", [128, 144])
            at = [0]

            def sm(n, dt=f32):
                v = small[:, at[0]:at[0] + n]
                at[0] += n
                return v if dt is f32 else v.bitcast(dt)

            smax, nmax, psums, rsums = sm(4), sm(4), sm(4), sm(4)
            q_ssq, q_ms, q_rms = sm(4), sm(4), sm(4)
            k_ssq, k_ms, k_rms = sm(4), sm(4), sm(4)
            neghalf = sm(4)
            bn_x, mv_x, eps_x = sm(6), sm(2), sm(1)
            bn_2, mv_2, ve_2, rstd_2 = sm(6), sm(2), sm(1), sm(1)
            wqk, qw_s, kw_s = sm(1), sm(1), sm(1)
            lg, top8, idx8, idxf = sm(E), sm(8), sm(8, u32), sm(2)
            mask = sm(E, bf16)
            posm, pos2, over = sm(2 * E), sm(2), sm(2)
            dst, tokf, toki = sm(2, i32), sm(1), sm(1, i32)
            list_off = sm(2)

            Q_B, K_B, V_B, S_B, PT_B, QT_B, OT_B, WO_B = pb

            d_w = [sem("d_w_even"), sem("d_w_odd")]
            d_small, d_c, d_x, d_xs, d_xr = sem("d_small"), sem("d_c"), sem("d_x"), sem("d_xs"), sem("d_xr")
            d_x1, d_xn2, d_sent = sem("d_x1_stored"), sem("d_xn2_stored"), sem("d_sentinel")
            s_mw, s_zero = sem("s_mw"), sem("s_zero")
            w_mean, w_cent, w_hi, w_lo = sem("w_mean"), sem("w_centred"), sem("w_hi"), sem("w_lo")
            wqk_done = sem("wqk_done")
            c_hi, c_lo, x_hi, x_lo = sem("c_hi"), sem("c_lo"), sem("x_hi"), sem("x_lo")
            k_done, v_done, q_done = sem("k_done"), sem("v_done"), sem("q_done")
            k_cp, k_sq, k_m, k_r, k_sc, k_tr, k_hi, k_lo = (sem(n) for n in (
                "k_copied", "k_squared", "k_meansq", "k_rms", "k_scaled", "k_transposed", "k_hi", "k_lo"))
            v_hi, v_lo = sem("v_hi"), sem("v_lo")
            q_cp, q_sq, q_m, q_r, q_tr, q_hi, q_lo = (sem(n) for n in (
                "q_copied", "q_squared", "q_meansq", "q_rms", "q_transposed", "q_hi", "q_lo"))
            sc_done, mx_done, nm_done, exp_done, rs_done, p_done = (sem(n) for n in (
                "scores_done", "max_done", "negmax_done", "exp_done", "rsum_done", "probs_done"))
            pt_done, pt_hi, pt_lo, ot_done, ot_hi, ot_lo = (sem(n) for n in (
                "pt_done", "pt_hi", "pt_lo", "ot_done", "ot_hi", "ot_lo"))
            wo_used, wo_done, x1_done, b2_done, mv2_done, ve2_done, r2_done, xn2_done = (sem(n) for n in (
                "wo_used", "wo_done", "x1_done", "bn2_done", "mv2_done", "ve2_done", "rstd2_done", "xn2_done"))
            bx_done, mvx_done, eps_done = sem("bnx_done"), sem("mvx_done"), sem("eps_done")
            xt_done, xt_cp, lg_done, lg_cp, t8, i8, ixf, mk = (sem(n) for n in (
                "xn2T_done", "xn2T_copied", "logits_done", "logits_copied", "top8_done", "idx8_done",
                "idxf_done", "mask_done"))
            pos_done, pm, p2, ov, ovb, d0, d1, dst_rdy, tok_i, tok_n, mac = (sem(n) for n in (
                "pos_done", "pos_masked", "pos_reduced", "over_done", "over_big", "dst_a", "dst_b",
                "dst_ready", "token_ids", "token_next", "macc_done"))

            block = ctx.enter_context(nc.Block())

            LOTS = [("k", 0), ("v", 0)] + [("q", n) for n in range(4)] + [("o", n) for n in range(4)]
            NLOT = len(LOTS)
            QLOT = 2

            def lot_parts(l):
                kind, n = LOTS[l]
                if kind == "k":
                    return [w[:, 0, :, :] for w in wkvp]
                if kind == "v":
                    return [w[:, 1, :, :] for w in wkvp]
                if kind == "q":
                    return [w[:, :, n * 512:(n + 1) * 512] for w in wqp]
                return [w[:, 4 * n:4 * n + 4, :] for w in wop]

            def stage(l):
                return work[:, 4 * (l % 2):4 * (l % 2) + 4, :]

            @block.sync
            def _(sp):
                sp.dma_start(gate[:, :, :], gateT).then_inc(d_small, 16)
                sp.dma_start(qw_s, qw).then_inc(d_small, 16)
                sp.dma_start(kw_s, kw).then_inc(d_small, 16)
                for l, (kind, n) in enumerate(LOTS):
                    if l >= 2:
                        sp.wait_ge(w_lo, l - 1)
                    if kind in "kv":
                        src = (wk if kind == "k" else wv).rearrange("(c p) n -> p c n", p=128)
                    elif kind == "q":
                        src = wq.rearrange("(c p) n -> p c n", p=128)[:, :, n * 512:(n + 1) * 512]
                    else:
                        src = wo.rearrange("(h p) n -> p h n", p=128)[:, 4 * n:4 * n + 4, :]
                    sp.dma_start(stage(l), src).then_inc(d_w[l % 2], 16)
                sp.wait_ge(s_const, 1)
                sp.dma_start(table_d[LIST1:, :].rearrange("(p c) o -> p (c o)", p=128),
                             sentinel).then_inc(d_sent, 16)
                sp.wait_ge(w_lo, NLOT)

                raw_v = raw.rearrange("p (c t) -> p c t", c=NC)

                def load_c(b):
                    wait(sp, x_lo, b)
                    sp.dma_start(raw_v, cT[b]).then_inc(d_c, 16)

                def load_x(b):
                    wait(sp, c_lo, b + 1)
                    sp.dma_start(raw_v, xT[b]).then_inc(d_x, 16)

                def load_stat(b):
                    wait(sp, bx_done, b)
                    sp.dma_start(x_stat, x[b]).then_inc(d_xs, 16)

                def load_res(b):
                    wait_apart(sp, (xn2_done, b), (d_x1, 16 * b))
                    sp.dma_start(x_res, x[b]).then_inc(d_xr, 16)

                def store_x1(b):
                    wait(sp, x1_done, b + 1)
                    sp.dma_start(x1_d[b], x_res).then_inc(d_x1, 16)

                def store_xn2(b):
                    wait_apart(sp, (xn2_done, b + 1))
                    sp.dma_start(xn2_d[bass.ds(b * 128, 128), :], xn2).then_inc(d_xn2, 16)

                load_c(0)
                load_stat(0)
                load_x(0)
                load_res(0)

                def body(b, first=False, last=False):
                    if not last:
                        load_c(b + 1)
                        load_stat(b + 1)
                    if not first:
                        store_x1(b - 1)
                    if not last:
                        load_x(b + 1)
                    if not first:
                        store_xn2(b - 1)
                        load_res(b)

                body(0, first=True)
                body(1)
                with sp.Fori(2, NB - 1) as b:
                    body(b)
                body(NB - 1, last=True)
                store_x1(NB - 1)
                store_xn2(NB - 1)
                sp.wait_ge(d_x1, 16 * NB)
                sp.wait_ge(d_xn2, 16 * NB)
                sp.wait_ge(d_sent, 16)

            @block.tensor
            def _(pe):
                pe.wait_ge(s_mw, 1)
                for n in range(4):
                    l = QLOT + n
                    pe.wait_ge(d_w[l % 2], 16 * (l // 2 + 1))
                    for c in range(NC):
                        last_mm = nc.tensor.matmul(pb[n][:, :], mean_w, stage(l)[:, c, :],
                                                   start=(c == 0), stop=(c == NC - 1))
                    last_mm.then_inc(w_mean, 1)

                PARTS = ((0, 0), (0, 1), (1, 0))

                def project(bank, lhs, rhs):
                    n = 0
                    for c in range(NC):
                        for a, b_ in PARTS:
                            mm = nc.tensor.matmul(bank[:, :], lhs[a][:, c, :], rhs[b_][:, c, :],
                                                  start=(n == 0), stop=(n == 3 * NC - 1))
                            n += 1
                    return mm

                def keys(b):
                    wait(pe, c_lo, b + 1)
                    wait(pe, lg_cp, b - 1)
                    wait(pe, k_lo, b)
                    project(K_B, cp, [w[:, 0, :, :] for w in wkvp]).then_inc(k_done, 1)

                def values(b):
                    wait(pe, v_lo, b)
                    project(V_B, cp, [w[:, 1, :, :] for w in wkvp]).then_inc(v_done, 1)

                def queries(b, g):
                    if g == 0:
                        wait(pe, x_lo, b + 1)
                    wait(pe, q_cp, 4 * b + g)
                    project(Q_B, xp, [w[:, :, g * 512:(g + 1) * 512] for w in wqp]).then_inc(q_done, 1)

                def transpose_q(b, g):
                    u = 4 * b + g
                    wait(pe, q_cp, u + 1)
                    wait(pe, q_lo, u)
                    for h in range(HPG):
                        tr = nc.tensor.transpose(QT_B[:, h * 128:(h + 1) * 128],
                                                 q_nat[:, h * 128:(h + 1) * 128], ident[:, :])
                    tr.then_inc(q_tr, 1)

                def transpose_k(b):
                    wait(pe, k_sc, b + 1)
                    for g in range(NG):
                        tr = nc.tensor.transpose(K_B[:, g * 128:(g + 1) * 128],
                                                 k_nat[:, g * 128:(g + 1) * 128], ident[:, :])
                    tr.then_inc(k_tr, 1)

                def scores(b, g):
                    u = 4 * b + g
                    if g == 0:
                        wait(pe, k_lo, b + 1)
                    wait(pe, q_lo, u + 1)
                    wait(pe, exp_done, u)
                    for h in range(HPG):
                        for n, (a, b_) in enumerate(PARTS):
                            mm = nc.tensor.matmul(S_B[:, h * 128:(h + 1) * 128], qp[a][:, h, :],
                                                  kp[b_][:, g, :], start=(n == 0), stop=(n == 2))
                    mm.then_inc(sc_done, 1)

                def transpose_p(b, g):
                    u = 4 * b + g
                    wait(pe, p_done, u + 1)
                    wait(pe, pt_lo, u)
                    for h in range(HPG):
                        tr = nc.tensor.transpose(PT_B[:, h * 128:(h + 1) * 128],
                                                 probs[:, h * 128:(h + 1) * 128], ident[:, :])
                    tr.then_inc(pt_done, 1)

                def attend(b, g):
                    u = 4 * b + g
                    wait(pe, v_lo, b + 1)
                    wait(pe, pt_lo, u + 1)
                    wait(pe, ot_lo, u)
                    if g == 3:
                        wait(pe, pos_read_count, b)
                    for n, (a, b_) in enumerate(PARTS):
                        mm = nc.tensor.matmul(OT_B[:, :], vp[a][:, g, :], ptp[b_][:, :, :],
                                              start=(n == 0), stop=(n == 2))
                    mm.then_inc(ot_done, 1)

                def out_project(b, g, half):
                    u = 4 * b + g
                    if half == 0:
                        wait(pe, ot_lo, u + 1)
                        if g == 0:
                            wait(pe, x1_done, b)
                    for h in (2 * half, 2 * half + 1):
                        for n, (a, b_) in enumerate(PARTS):
                            mm = nc.tensor.matmul(WO_B[:, :], otp[a][:, h, :], wop[b_][:, g * HPG + h, :],
                                                  start=(g == 0 and h == 0 and n == 0),
                                                  stop=(g == NG - 1 and h == HPG - 1 and n == 2))
                    if half == 1:
                        mm.then_inc(wo_used, 1)

                def transpose_x(b):
                    wait(pe, xn2_done, b + 1)
                    wait(pe, k_lo, b + 2)
                    for c in range(NC):
                        tr = nc.tensor.transpose(K_B[:, c * 128:(c + 1) * 128],
                                                 xn2[:, c * 128:(c + 1) * 128], ident[:, :])
                    tr.then_inc(xt_done, 1)

                def route(b):
                    wait(pe, xt_cp, b + 1)
                    for c in range(NC):
                        mm = nc.tensor.matmul(K_B[:, 0:E], xn2T[:, c * 128:(c + 1) * 128], gate[:, c, :],
                                              start=(c == 0), stop=(c == NC - 1))
                    mm.then_inc(lg_done, 1)

                def positions(b):
                    wait(pe, mk, b + 1)
                    wait(pe, mac, b + 1)
                    wait(pe, ot_lo, 4 * b + 7)
                    nc.tensor.matmul(OT_B[:, 0:2 * E], tri[:, :], mask, start=True, stop=False)
                    nc.tensor.matmul(OT_B[:, 0:2 * E], ones_b[:, :], macc[:, :],
                                     start=False, stop=True).then_inc(pos_done, 1)

                pos_read_count = pm
                pe.wait_ge(s_const, 1)
                pe.wait_ge(d_small, 48)
                pe.wait_ge(w_lo, NLOT)
                keys(0)
                values(0)
                queries(0, 0)
                transpose_k(0)
                transpose_q(0, 0)

                def body(b, first=False, last=False):
                    for g in range(NG):
                        has_prev = not (first and g == 0)
                        has_next = not (last and g == NG - 1)
                        prev = (b, g - 1) if g else (b - 1, NG - 1)
                        nxt = (b, g + 1) if g < NG - 1 else (b + 1, 0)
                        scores(b, g)
                        if has_prev:
                            attend(*prev)
                        if g == 3 and not last:
                            keys(b + 1)
                            values(b + 1)
                        if has_next:
                            queries(*nxt)
                        if g == 2 and not first:
                            transpose_x(b - 1)
                        if has_prev:
                            out_project(*prev, 0)
                        transpose_p(b, g)
                        if has_next:
                            transpose_q(*nxt)
                        if g == 3 and not last:
                            transpose_k(b + 1)
                        if g == 2 and not first:
                            route(b - 1)
                        if g == 3 and not first:
                            positions(b - 1)
                        if has_prev:
                            out_project(*prev, 1)

                body(0, first=True)
                body(1)
                with pe.Fori(2, NB - 1) as b:
                    body(b)
                body(NB - 1, last=True)
                attend(NB - 1, NG - 1)
                out_project(NB - 1, NG - 1, 0)
                out_project(NB - 1, NG - 1, 1)
                pe.wait_ge(xn2_done, NB)
                for c in range(NC):
                    tr = nc.tensor.transpose(K_B[:, c * 128:(c + 1) * 128],
                                             xn2[:, c * 128:(c + 1) * 128], ident[:, :])
                tr.then_inc(xt_done, 1)
                route(NB - 1)
                pe.wait_ge(mk, NB)
                pe.wait_ge(mac, NB)
                pe.wait_ge(ot_lo, NU)
                nc.tensor.matmul(OT_B[:, 0:2 * E], tri[:, :], mask, start=True, stop=False)
                nc.tensor.matmul(OT_B[:, 0:2 * E], ones_b[:, :], macc[:, :],
                                 start=False, stop=True).then_inc(pos_done, 1)

            @block.scalar
            def _(act):
                for l, (kind, n) in enumerate(LOTS):
                    if kind == "q":
                        act.wait_ge(w_cent, l - QLOT + 1)
                    else:
                        act.wait_ge(d_w[l % 2], 16 * (l // 2 + 1))
                    nc.scalar.copy(lot_parts(l)[0], stage(l)).then_inc(w_hi, 1)

                raw_v = raw.rearrange("p (c t) -> p c t", c=NC)

                def split_c(b):
                    wait(act, d_c, 16 * (b + 1))
                    wait(act, v_done, b)
                    nc.scalar.copy(cp[0][:, :, :], raw_v).then_inc(c_hi, 1)

                def split_x(b):
                    wait(act, d_x, 16 * (b + 1))
                    wait(act, q_done, 4 * b)
                    nc.scalar.copy(xp[0][:, :, :], raw_v).then_inc(x_hi, 1)

                def copy_k(b):
                    wait(act, k_done, b + 1)
                    wait(act, k_tr, b)
                    wait(act, lg_done, b - 1)
                    nc.scalar.copy(k_nat, K_B[:, :]).then_inc(k_cp, 1)

                def split_k(b):
                    wait(act, k_tr, b + 1)
                    wait(act, sc_done, 4 * b)
                    if isinstance(b, int) and b == 0:
                        act.wait_ge(wqk_done, 1)
                    nc.scalar.activation(kp[0][:, :, :], K_B[:, :].rearrange("p (g t) -> p g t", g=NG),
                                         ACT.Copy, scale=wqk).then_inc(k_hi, 1)

                def split_v(b):
                    wait(act, v_done, b + 1)
                    wait(act, ot_done, 4 * b)
                    nc.scalar.copy(vp[0][:, :, :], V_B[:, :].rearrange("p (g t) -> p g t", g=NG)).then_inc(v_hi, 1)

                def copy_q(b, g):
                    u = 4 * b + g
                    wait(act, q_done, u + 1)
                    wait(act, q_tr, u)
                    wait(act, q_sq, u)
                    nc.scalar.copy(q_nat, Q_B[:, :]).then_inc(q_cp, 1)

                def split_q(b, g):
                    u = 4 * b + g
                    wait(act, q_tr, u + 1)
                    wait(act, sc_done, u)
                    nc.scalar.copy(qp[0][:, :, :], QT_B[:, :].rearrange("p (h t) -> p h t", h=HPG)).then_inc(q_hi, 1)

                def exps(b, g):
                    u = 4 * b + g
                    wait(act, nm_done, u + 1)
                    wait(act, pt_done, u)
                    for h in range(HPG):
                        ex = nc.scalar.activation(probs[:, h * 128:(h + 1) * 128], S_B[:, h * 128:(h + 1) * 128],
                                                  ACT.Exp, bias=nmax[:, h:h + 1], scale=q_rms[:, h:h + 1],
                                                  accum_out=psums[:, h:h + 1])
                    ex.then_inc(exp_done, 1)

                def split_p(b, g):
                    u = 4 * b + g
                    wait(act, pt_done, u + 1)
                    wait(act, ot_done, u)
                    nc.scalar.copy(ptp[0][:, :, :], PT_B[:, :].rearrange("p (h t) -> p h t", h=HPG)).then_inc(pt_hi, 1)

                def split_o(b, g):
                    u = 4 * b + g
                    wait(act, ot_done, u + 1)
                    wait(act, wo_used, u)
                    nc.scalar.copy(otp[0][:, :, :], OT_B[:, :].rearrange("p (h t) -> p h t", h=HPG)).then_inc(ot_hi, 1)

                def copy_xt(b, keys_after=True):
                    wait(act, xt_done, b + 1)
                    if keys_after:
                        wait(act, k_tr, b + 2)
                    nc.scalar.copy(xn2T, K_B[:, :]).then_inc(xt_cp, 1)

                act.wait_ge(w_lo, NLOT)
                split_c(0)
                split_x(0)
                copy_k(0)
                copy_q(0, 0)
                split_k(0)
                split_q(0, 0)

                def body(b, first=False, last=False):
                    for g in range(NG):
                        prev = (b, g - 1) if g else (b - 1, NG - 1)
                        nxt = (b, g + 1) if g < NG - 1 else (b + 1, 0)
                        if not (first and g == 0):
                            split_o(*prev)
                        if g == 0:
                            split_v(b)
                        exps(b, g)
                        if g == 1 and not last:
                            split_c(b + 1)
                        if g == 3 and not last:
                            split_x(b + 1)
                            copy_k(b + 1)
                        if not (last and g == NG - 1):
                            copy_q(*nxt)
                        if g == 2 and not first:
                            copy_xt(b - 1)
                        split_p(b, g)
                        if not (last and g == NG - 1):
                            split_q(*nxt)
                        if g == 3 and not last:
                            split_k(b + 1)

                body(0, first=True)
                body(1)
                with act.Fori(2, NB - 1) as b:
                    body(b)
                body(NB - 1, last=True)
                split_o(NB - 1, NG - 1)
                copy_xt(NB - 1, keys_after=False)

            @block.vector
            def _(dve):
                def minus(part, whole):
                    return nc.vector.tensor_tensor(part[1], whole, part[0].bitcast(f32), ALU.subtract)

                nc.vector.memset(mean_w, 1.0 / HID).then_inc(s_mw, 1)
                nc.vector.memset(neghalf, -0.5)
                nc.vector.memset(macc[:, :], 0.0)
                nc.vector.memset(list_off[:, 0:1], 0.0)
                nc.vector.memset(list_off[:, 1:2], float(LIST1)).then_inc(mac, 1)
                dve.wait_ge(d_small, 48)
                nc.vector.tensor_tensor(wqk, qw_s, kw_s, ALU.mult).then_inc(wqk_done, 1)
                for l, (kind, n) in enumerate(LOTS):
                    if kind == "q":
                        dve.wait_ge(w_mean, n + 1)
                        nc.vector.tensor_tensor(stage(l), stage(l),
                                                pb[n][:, None, :].broadcast_to([128, NC, 512]),
                                                ALU.subtract).then_inc(w_cent, 1)
                    dve.wait_ge(w_hi, l + 1)
                    hi, lo = lot_parts(l)
                    nc.vector.tensor_tensor(lo, stage(l), hi.bitcast(f32), ALU.subtract).then_inc(w_lo, 1)

                raw_v = raw.rearrange("p (c t) -> p c t", c=NC)

                def view(bank, n=4):
                    return bank[:, :].rearrange("p (h t) -> p h t", h=n)

                def all3(parts):
                    return [p[:, :, :] for p in parts]

                def split_c(b):
                    wait(dve, c_hi, b + 1)
                    minus(all3(cp), raw_v).then_inc(c_lo, 1)

                def split_x(b):
                    wait(dve, x_hi, b + 1)
                    minus(all3(xp), raw_v).then_inc(x_lo, 1)

                def stats_x(b):
                    wait(dve, d_xs, 16 * (b + 1))
                    wait(dve, mvx_done, b)
                    nc.vector.bn_stats(bn_x, x_stat).then_inc(bx_done, 1)
                    wait(dve, bx_done, b + 1, apart=True)
                    wait(dve, eps_done, b)
                    nc.vector.bn_aggr(mv_x, bn_x).then_inc(mvx_done, 1)

                def square_k(b):
                    wait(dve, k_cp, b + 1)
                    wait(dve, k_m, b)
                    wait(dve, q_sq, 4 * b)
                    for g in range(NG):
                        kk = k_nat[:, g * 128:(g + 1) * 128]
                        sq = nc.vector.tensor_tensor_reduce(out=junk[:, g, :], in0=kk, in1=kk, scale=1.0, scalar=0.0,
                                                            op0=ALU.mult, op1=ALU.add, accum_out=k_ssq[:, g:g + 1])
                    sq.then_inc(k_sq, 1)

                def scale_k(b):
                    wait(dve, k_r, b + 1)
                    kv = k_nat.rearrange("p (g t) -> p g t", g=NG)
                    nc.vector.tensor_tensor(kv, kv, k_rms[:, :, None].broadcast_to([128, NG, 128]),
                                            ALU.mult).then_inc(k_sc, 1)

                def split_k(b):
                    wait(dve, k_hi, b + 1)
                    nc.vector.scalar_tensor_tensor(out=kp[1][:, :, :], in0=view(K_B), scalar=wqk,
                                                   in1=kp[0][:, :, :].bitcast(f32), op0=ALU.mult,
                                                   op1=ALU.subtract).then_inc(k_lo, 1)

                def split_v(b):
                    wait(dve, v_hi, b + 1)
                    minus(all3(vp), view(V_B)).then_inc(v_lo, 1)

                def square_q(b, g):
                    u = 4 * b + g
                    wait(dve, q_cp, u + 1)
                    wait(dve, q_m, u)
                    if g == 0:
                        wait(dve, k_sq, b + 1)
                    for h in range(HPG):
                        qq = q_nat[:, h * 128:(h + 1) * 128]
                        sq = nc.vector.tensor_tensor_reduce(out=junk[:, h, :], in0=qq, in1=qq, scale=1.0, scalar=0.0,
                                                            op0=ALU.mult, op1=ALU.add, accum_out=q_ssq[:, h:h + 1])
                    sq.then_inc(q_sq, 1)

                def split_q(b, g):
                    wait(dve, q_hi, 4 * b + g + 1)
                    minus(all3(qp), view(QT_B)).then_inc(q_lo, 1)

                def maxima(b, g):
                    u = 4 * b + g
                    wait(dve, sc_done, u + 1)
                    nc.vector.tensor_reduce(smax, view(S_B), AX.X, ALU.max).then_inc(mx_done, 1)
                    wait(dve, mx_done, u + 1)
                    wait(dve, q_r, u + 1)
                    wait(dve, exp_done, u)
                    nc.vector.scalar_tensor_tensor(out=nmax, in0=smax, scalar=-1.0, in1=q_rms,
                                                   op0=ALU.mult, op1=ALU.mult).then_inc(nm_done, 1)

                def normalise(b, g):
                    u = 4 * b + g
                    wait(dve, exp_done, u + 1)
                    wait(dve, p_done, u)
                    nc.vector.reciprocal(rsums, psums).then_inc(rs_done, 1)
                    wait(dve, rs_done, u + 1)
                    pv = probs.rearrange("p (h t) -> p h t", h=HPG)
                    nc.vector.tensor_tensor(pv, pv, rsums[:, :, None].broadcast_to([128, HPG, 128]),
                                            ALU.mult).then_inc(p_done, 1)

                def split_p(b, g):
                    wait(dve, pt_hi, 4 * b + g + 1)
                    minus(all3(ptp), view(PT_B)).then_inc(pt_lo, 1)

                def split_o(b, g):
                    wait(dve, ot_hi, 4 * b + g + 1)
                    minus(all3(otp), view(OT_B)).then_inc(ot_lo, 1)

                def residual(b):
                    wait(dve, wo_used, 4 * b + 4)
                    wait(dve, d_xr, 16 * (b + 1))
                    nc.vector.tensor_tensor(x_res, x_res, WO_B[:, :], ALU.add).then_inc(x1_done, 1)
                    wait(dve, x1_done, b + 1)
                    nc.vector.bn_stats(bn_2, x_res).then_inc(b2_done, 1)
                    wait(dve, b2_done, b + 1, apart=True)
                    wait(dve, ve2_done, b)
                    wait(dve, xn2_done, b)
                    nc.vector.bn_aggr(mv_2, bn_2).then_inc(mv2_done, 1)

                def norm2(b):
                    wait(dve, r2_done, b + 1)
                    wait(dve, d_xn2, 16 * b)
                    wait(dve, xt_done, b)
                    nc.vector.tensor_scalar(xn2, x_res, mv_2[:, 0:1], rstd_2, ALU.subtract,
                                            ALU.mult).then_inc(xn2_done, 1)

                def choose(b):
                    wait(dve, lg_done, b + 1)
                    nc.vector.tensor_copy(lg, K_B[:, 0:E]).then_inc(lg_cp, 1)
                    wait(dve, lg_cp, b + 1, apart=True)
                    nc.vector.max(top8, lg).then_inc(t8, 1)
                    wait(dve, t8, b + 1, apart=True)
                    nc.vector.max_index(idx8, top8, lg).then_inc(i8, 1)
                    wait(dve, i8, b + 1)
                    nc.vector.tensor_copy(idxf, idx8[:, 0:2]).then_inc(ixf, 1)
                    nc.vector.tensor_tensor(tab[:, bass.ds(b * TABW + 4, 1)], top8[:, 1:2], top8[:, 0:1], ALU.subtract)
                    wait(dve, ixf, b + 1)
                    wait(dve, pos_done, b)
                    nc.vector.tensor_tensor(mask.rearrange("p (k e) -> p k e", k=2),
                                            iota12[:, None, :].broadcast_to([128, 2, E]),
                                            idxf[:, :, None].broadcast_to([128, 2, E]),
                                            ALU.is_equal).then_inc(mk, 1)
                    nc.vector.tensor_copy(tab[:, bass.ds(b * TABW, 2)], idxf)

                def place(b):
                    wait(dve, pos_done, b + 1)
                    nc.vector.tensor_tensor(posm, OT_B[:, 0:2 * E], mask, ALU.mult).then_inc(pm, 1)
                    wait(dve, mac, b + 1)
                    nc.vector.tensor_tensor(macc[:, :], macc[:, :], mask, ALU.add).then_inc(mac, 1)
                    wait(dve, pm, b + 1)
                    nc.vector.tensor_reduce(pos2, posm.rearrange("p (k e) -> p k e", k=2), AX.X,
                                            ALU.add).then_inc(p2, 1)
                    wait(dve, p2, b + 1)
                    nc.vector.tensor_scalar(over, pos2, float(CAP), float(BIG), ALU.is_ge, ALU.mult).then_inc(ov, 1)
                    nc.vector.tensor_copy(tab[:, bass.ds(b * TABW + 2, 2)], pos2)
                    wait(dve, ov, b + 1)
                    nc.vector.tensor_tensor(over, over, pos2, ALU.add).then_inc(ovb, 1)
                    wait(dve, ovb, b + 1)
                    nc.vector.scalar_tensor_tensor(out=over[:, 0:1], in0=idxf[:, 0:1], scalar=float(STRIDE),
                                                   in1=over[:, 0:1], op0=ALU.mult, op1=ALU.add)
                    nc.vector.scalar_tensor_tensor(out=over[:, 1:2], in0=idxf[:, 1:2], scalar=float(CP),
                                                   in1=over[:, 1:2], op0=ALU.mult, op1=ALU.add).then_inc(d0, 1)
                    wait(dve, d0, b + 1)
                    wait(dve, s_table, 32 * b)
                    nc.vector.tensor_tensor(dst, over, list_off, ALU.add).then_inc(dst_rdy, 1)
                    wait(dve, tok_n, b)
                    nc.vector.tensor_copy(toki, tokf).then_inc(tok_i, 1)
                    wait(dve, tok_i, b + 1)
                    nc.vector.tensor_scalar(tokf, tokf, 128.0, None, ALU.add).then_inc(tok_n, 1)

                dve.wait_ge(s_const, 1)
                dve.wait_ge(d_sent, 16)
                split_c(0)
                split_x(0)
                stats_x(0)
                square_k(0)
                square_q(0, 0)
                scale_k(0)
                split_k(0)
                split_q(0, 0)

                def body(b, first=False, last=False):
                    for g in range(NG):
                        prev = (b, g - 1) if g else (b - 1, NG - 1)
                        nxt = (b, g + 1) if g < NG - 1 else (b + 1, 0)
                        maxima(b, g)
                        if not (first and g == 0):
                            split_o(*prev)
                        if g == 0:
                            split_v(b)
                        if g == 2 and not first:
                            norm2(b - 1)
                        if g == 3 and not first:
                            choose(b - 1)
                        normalise(b, g)
                        if g == 1 and not first:
                            residual(b - 1)
                        if g == 1 and not last:
                            split_c(b + 1)
                        if g == 3 and not last:
                            split_x(b + 1)
                            stats_x(b + 1)
                            square_k(b + 1)
                        if not (last and g == NG - 1):
                            square_q(*nxt)
                        if g == 3 and not last:
                            scale_k(b + 1)
                        split_p(b, g)
                        if not (last and g == NG - 1):
                            split_q(*nxt)
                        if g == 3 and not last:
                            split_k(b + 1)
                        if g == 3 and not first:
                            place(b - 1)

                body(0, first=True)
                body(1)
                with dve.Fori(2, NB - 1) as b:
                    body(b)
                body(NB - 1, last=True)
                split_o(NB - 1, NG - 1)
                residual(NB - 1)
                norm2(NB - 1)
                choose(NB - 1)
                place(NB - 1)

            @block.gpsimd
            def _(pool):
                nc.gpsimd.memset(ident[:, :], 0.0)
                nc.gpsimd.memset(ones_b[:, :], 1.0)
                nc.gpsimd.memset(tri[:, :], 1.0)
                nc.gpsimd.iota(iota12[:, :], pattern=[[1, E]], base=0, channel_multiplier=0,
                               allow_small_or_imprecise_dtypes=True)
                nc.gpsimd.iota(tokf, pattern=[[0, 1]], base=0, channel_multiplier=1,
                               allow_small_or_imprecise_dtypes=True)
                nc.gpsimd.iota(sentinel, pattern=[[0, E * CP // 128]], base=BIG,
                               channel_multiplier=0).then_inc(s_zero, 1)
                pool.wait_ge(s_zero, 1)
                nc.gpsimd.affine_select(out=ident[:, :], in_=ident[:, :], compare_op=ALU.not_equal, fill=1.0,
                                        base=0, pattern=[[-1, 128]], channel_multiplier=1)
                nc.gpsimd.affine_select(out=tri[:, :], in_=tri[:, :], compare_op=ALU.is_gt, fill=0.0,
                                        base=0, pattern=[[1, 128]], channel_multiplier=-1).then_inc(s_const, 1)

                def eps_of_x(b):
                    wait(pool, mvx_done, b + 1, apart=True)
                    nc.gpsimd.tensor_scalar(eps_x, mv_x[:, 1:2], HD * ATTN_EPS, HD * ATTN_EPS * LN_EPS,
                                            ALU.mult, ALU.add).then_inc(eps_done, 1)

                def rms_k(b):
                    wait(pool, k_sq, b + 1, apart=True)
                    nc.gpsimd.tensor_scalar(k_ms, k_ssq, 1.0 / HD, ATTN_EPS, ALU.mult, ALU.add).then_inc(k_m, 1)
                    wait(pool, k_m, b + 1)
                    wait(pool, k_sc, b)
                    nc.gpsimd.tensor_tensor(k_rms, k_ms, neghalf, ALU.pow).then_inc(k_r, 1)

                def rms_q(b, g):
                    u = 4 * b + g
                    wait(pool, q_sq, u + 1)
                    if g == 0:
                        wait(pool, eps_done, b + 1)
                    nc.gpsimd.tensor_tensor(q_ms, q_ssq, eps_x.broadcast_to([128, HPG]), ALU.add).then_inc(q_m, 1)
                    wait(pool, q_m, u + 1)
                    wait(pool, exp_done, u)
                    nc.gpsimd.tensor_tensor(q_rms, q_ms, neghalf, ALU.pow).then_inc(q_r, 1)

                def rstd2(b):
                    wait(pool, mv2_done, b + 1, apart=True)
                    nc.gpsimd.tensor_scalar(ve_2, mv_2[:, 1:2], LN_EPS, None, ALU.add).then_inc(ve2_done, 1)
                    wait(pool, ve2_done, b + 1)
                    wait(pool, xn2_done, b)
                    nc.gpsimd.tensor_tensor(rstd_2, ve_2, neghalf[:, 0:1], ALU.pow).then_inc(r2_done, 1)

                def scatter(b):
                    wait_apart(pool, (dst_rdy, b + 1), (tok_i, b + 1))
                    for k in range(2):
                        nc.gpsimd.indirect_dma_start(
                            out=table_d, out_offset=bass.IndirectOffsetOnAxis(ap=dst[:, k:k + 1], axis=0),
                            in_=toki, in_offset=None, bounds_check=E * STRIDE + E * CP - 1,
                            oob_is_err=False).then_inc(s_table, 16)

                pool.wait_ge(mac, 1)
                pool.wait_ge(d_sent, 16)
                eps_of_x(0)
                rms_k(0)
                rms_q(0, 0)

                def body(b, first=False, last=False):
                    for g in range(NG):
                        nxt = (b, g + 1) if g < NG - 1 else (b + 1, 0)
                        if g == 3 and not last:
                            eps_of_x(b + 1)
                            rms_k(b + 1)
                        if g == 1 and not first:
                            rstd2(b - 1)
                        if not (last and g == NG - 1):
                            rms_q(*nxt)
                        if g == 3 and not first:
                            scatter(b - 1)

                body(0, first=True)
                body(1)
                with pool.Fori(2, NB - 1) as b:
                    body(b)
                body(NB - 1, last=True)
                rstd2(NB - 1)
                scatter(NB - 1)
                pool.wait_ge(s_table, 32 * NB)

        experts(nc, gt=dict(wait=wait, wait_apart=wait_apart, sem=sem, pb=pb, ident=ident, ones_b=ones_b, tab=tab, iota12=iota12,
                            macc=macc, x1_d=x1_d, xn2_d=xn2_d, table_d=table_d, y_d=y_d, LIST1=LIST1),
                w13=w13, w2T=w2T, out=out)
    return nc


def kernel(x, ctx_2048, L0_xattn_Wq, L0_xattn_Wk, L0_xattn_Wv, L0_xattn_Wo, L0_xattn_q_norm_w,
           L0_xattn_k_norm_w, L0_ffn_gate_w, L0_ffn_w1, L0_ffn_w2, L0_ffn_w3):
    import concourse.bacc as bacc
    from concourse.bass_utils import run_bass_kernel_spmd

    def by_width(a):
        a = np.asarray(a)
        return np.ascontiguousarray(a.reshape(NB, SEQ, NC, 128).transpose(0, 3, 2, 1))

    def pieces(a):
        return np.ascontiguousarray(a.reshape(NC, 128, -1).transpose(1, 0, 2))

    w1, w2, w3 = (np.asarray(a) for a in (L0_ffn_w1, L0_ffn_w2, L0_ffn_w3))
    w13 = np.concatenate([w1, w3], axis=1).transpose(0, 2, 1)
    w13 = np.ascontiguousarray(w13.reshape(E, NC, 128, 2 * F).transpose(0, 2, 1, 3))
    arrays = {
        "x": np.ascontiguousarray(x), "xT": by_width(x), "cT": by_width(ctx_2048),
        "wq": np.ascontiguousarray(L0_xattn_Wq), "wk": np.ascontiguousarray(L0_xattn_Wk),
        "wv": np.ascontiguousarray(L0_xattn_Wv), "wo": np.ascontiguousarray(L0_xattn_Wo),
        "qw": np.asarray(L0_xattn_q_norm_w).reshape(HD, 1), "kw": np.asarray(L0_xattn_k_norm_w).reshape(HD, 1),
        "gateT": pieces(np.asarray(L0_ffn_gate_w).T), "w13": w13,
        "w2T": np.ascontiguousarray(w2.transpose(0, 2, 1)),
    }
    nc = bacc.Bacc("TRN2", target_bir_lowering=False, num_devices=1)
    aps = {n: nc.dram_tensor(n, a.shape, mybir.dt.from_np(a.dtype), kind="ExternalInput").ap()
           for n, a in arrays.items()}
    out = nc.dram_tensor("out", (NB, SEQ, HID), mybir.dt.float32, kind="ExternalOutput").ap()
    build(nc, out=out, **aps)
    result = run_bass_kernel_spmd(nc, [arrays], core_ids=[0])
    return result.results[0]["out"]
```

```python
from contextlib import ExitStack

import numpy as np

import concourse.bass as bass
from concourse import mybir
from concourse.alu_op_type import AluOpType as ALU

NB, SEQ, HID = 64, 128, 512
NH, NG, HD = 16, 4, 128
HPG = NH // NG
NC = HID // 128
NU = NB * NG
T = NB * SEQ
E, F = 12, 64
CAP = -(-T * 5 // (4 * E))
NT = -(-CAP // 128)
CP = NT * 128
STRIDE = 2 * CP
LIST1 = E * STRIDE
SPARE = LIST1 + E * CP
BIG = 1 << 20
ATTN_EPS, LN_EPS = 1e-6, 1e-5


def experts(nc, gt, w13, w2T, out):
    f32, i32 = mybir.dt.float32, mybir.dt.int32
    ACT = mybir.ActivationFunctionType
    wait, wait_apart, sem, pb, ident, ones_b, macc, xn2_d, table_d = (gt[k] for k in (
        "wait", "wait_apart", "sem", "pb", "ident", "ones_b", "macc", "xn2_d", "table_d"))

    with ExitStack() as ctx:
        tot = ctx.enter_context(nc.sbuf_tensor("tot", [128, E], f32))
        first_n = ctx.enter_context(nc.sbuf_tensor("first_n", [128, E], i32))
        s_tot, s_min, s_n = sem("totals_done"), sem("totals_clipped"), sem("first_n_done")
        d_join = [sem("d_joined_even"), sem("d_joined_odd")]
        d_tail = sem("d_tail")
        block = ctx.enter_context(nc.Block())

        @block.tensor
        def _(pe):
            nc.tensor.matmul(pb[0][:, 0:2 * E], ones_b[:, :], macc[:, :], start=True, stop=True).then_inc(s_tot, 1)

        @block.vector
        def _(dve):
            dve.wait_ge(s_tot, 1)
            nc.vector.tensor_scalar(tot[:, :], pb[0][:, 0:E], float(CAP), None, ALU.min).then_inc(s_min, 1)
            dve.wait_ge(s_min, 1)
            nc.vector.tensor_copy(first_n[:, :], tot[:, :]).then_inc(s_n, 1)

        def join(eng, p):
            eng.wait_ge(s_n, 1)
            for e in range(p, E, 2):
                n = eng.value_load(first_n[0:1, e:e + 1], min_val=0, max_val=CAP)
                eng.dma_start(table_d[bass.ds(n + e * STRIDE, CP), :],
                              table_d[LIST1 + e * CP:LIST1 + (e + 1) * CP, :]).then_inc(d_join[p], 16)

        @block.scalar
        def _(act):
            join(act, 1)

        @block.sync
        def _(sp):
            join(sp, 0)
            for p in range(2):
                sp.wait_ge(d_join[p], 16 * (E // 2))
            sp.dma_start(table_d[0:E * STRIDE, :].rearrange("(e s) o -> e s o", e=E)[:, CAP:CP, :],
                         table_d[SPARE + CAP:SPARE + CP, :][None, :, :].broadcast_to([E, CP - CAP, 2])
                         ).then_inc(d_tail, 16)
            sp.wait_ge(d_tail, 16)

    with ExitStack() as ctx:
        def sb(name, shape, dt=f32):
            return ctx.enter_context(nc.sbuf_tensor(name, shape, dt))

        w13_s = [sb(f"w13_{i}", [128, NC, 2 * F]) for i in range(2)]
        w2_s = [sb(f"w2_{i}", [F, HID]) for i in range(2)]
        from_i = [sb(f"from_{i}", [128, NT, 2], i32) for i in range(2)]
        to_i = [sb(f"to_{i}", [128, NT, 2], i32) for i in range(2)]
        xg = [sb(f"xg_{i}", [128, NT, HID]) for i in range(2)]
        xgT = sb("xgT", [128, NC, CP])
        h3, g13, eg, hT = (sb(nm, [F, CP]) for nm in ("h3", "g13", "eg", "hT"))
        yb = [sb(f"yb_{i}", [128, NT, HID]) for i in range(2)]
        d_w = [sem(f"d_expert_w{i}") for i in range(2)]
        d_from = [sem(f"d_from{i}") for i in range(2)]
        d_to = [sem(f"d_to{i}") for i in range(2)]
        d_g = [sem(f"d_gathered{i}") for i in range(2)]
        d_add = [sem(f"d_added{i}") for i in range(2)]
        w_used = [sem(f"expert_w_used{i}") for i in range(2)]
        xg_used = [sem(f"xg_used{i}") for i in range(2)]
        s_z = sem("xg_zeroed")
        tr_done = [sem("xg_tr_even"), sem("xg_tr_odd")]
        ev_done = [sem("xgT_even"), sem("xgT_odd")]
        y_done = [sem("y_even"), sem("y_odd")]
        yev_done = [sem("yb_even"), sem("yb_odd")]
        h_done, h3_done, g_done, e_done, dn_done, rc_done, hs_done, hT_used = (sem(nm) for nm in (
            "h_done", "h3_copied", "g13_done", "exp_g_done", "den_done", "recip_done", "h_silu_done", "hT_used"))
        block = ctx.enter_context(nc.Block())
        HALF = [(0, 512), (512, CP)]
        CNT = [(NT + 1) // 2, NT // 2]
        PAIRS = E // 2

        @block.sync
        def _(sp):
            def entries(e):
                return table_d[bass.ds(e * STRIDE, CP), :].rearrange("(p t) o -> p t o", t=NT)

            def load(j, i):
                e = 2 * j + i
                wait_apart(sp, (d_g[i], 16 * NT * j))
                sp.dma_start(from_i[i][:, :, :], entries(e)).then_inc(d_from[i], 16)
                wait(sp, w_used[i], j)
                sp.dma_start(w13_s[i][:, :, :], w13[e]).then_inc(d_w[i], 16)
                sp.dma_start(w2_s[i][:, :], w2T[e]).then_inc(d_w[i], 16)
                wait_apart(sp, (d_add[i], 16 * NT * j))
                sp.dma_start(to_i[i][:, :, :], entries(e)).then_inc(d_to[i], 16)

            load(0, 0)
            load(0, 1)
            with sp.Fori(1, PAIRS) as j:
                load(j, 0)
                load(j, 1)

        @block.gpsimd
        def _(pool):
            def gather(j, i):
                wait_apart(pool, (d_from[i], 16 * j + 16), (xg_used[i], j))
                for t in range(NT):
                    nc.gpsimd.indirect_dma_start(
                        out=xg[i][:, t, :], out_offset=None, in_=xn2_d,
                        in_offset=bass.IndirectOffsetOnAxis(ap=from_i[i][:, t, 0:1], axis=0),
                        bounds_check=T - 1, oob_is_err=False).then_inc(d_g[i], 16)

            def scatter_add(j, i):
                e = 2 * j + i
                wait_apart(pool, (d_to[i], 16 * j + 16), (d_add[1 - i], 16 * NT * (j + i)))
                for t in range(NT):
                    wait_apart(pool, (yev_done[t % 2], CNT[t % 2] * e + t // 2 + 1))
                    nc.gpsimd.indirect_dma_start(
                        out=out, out_offset=bass.IndirectOffsetOnAxis(ap=to_i[i][:, t, 0:1], axis=0),
                        in_=yb[i][:, t, :], in_offset=None, compute_op=ALU.add).then_inc(d_add[i], 16)

            for i in range(2):
                nc.gpsimd.memset(xg[i][:, :, :], 0.0).then_inc(s_z, 1)
            pool.wait_ge(s_z, 2)
            gather(0, 0)
            gather(0, 1)
            scatter_add(0, 0)
            gather(1, 0)
            scatter_add(0, 1)
            gather(1, 1)
            with pool.Fori(1, PAIRS - 1) as j:
                scatter_add(j, 0)
                gather(j + 1, 0)
                scatter_add(j, 1)
                gather(j + 1, 1)
            scatter_add(PAIRS - 1, 0)
            scatter_add(PAIRS - 1, 1)
            for i in range(2):
                pool.wait_ge(d_add[i], 16 * NT * PAIRS)

        @block.tensor
        def _(pe):
            def transposes(j, i):
                e = 2 * j + i
                pe.wait_ge(d_g[i], 16 * NT * (j + 1))
                for t in range(NT):
                    p = t % 2
                    wait(pe, ev_done[p], CNT[p] * e + t // 2)
                    for c in range(NC):
                        tr = nc.tensor.transpose(pb[p][:, c * 128:(c + 1) * 128],
                                                 xg[i][:, t, c * 128:(c + 1) * 128], ident[:, :])
                    tr.then_inc(tr_done[p], 1)
                pe.wait_ge(tr_done[(NT - 1) % 2], CNT[(NT - 1) % 2] * (e + 1))
                pe.sem_inc(xg_used[i], 1)

            def up(j, i):
                e = 2 * j + i
                pe.wait_ge(d_w[i], 32 * (j + 1))
                for p in range(2):
                    pe.wait_ge(ev_done[p], CNT[p] * (e + 1))
                for k, (lo, hi) in enumerate(HALF):
                    wait(pe, g_done, 2 * e)
                    for c in range(NC):
                        mm = nc.tensor.matmul(pb[2 + k][:, 0:hi - lo], w13_s[i][:, c, :], xgT[:, c, lo:hi],
                                              start=(c == 0), stop=(c == NC - 1))
                    mm.then_inc(h_done, 1)

            def down(j, i):
                e = 2 * j + i
                pe.wait_ge(hs_done, e + 1)
                for t in range(NT):
                    p = t % 2
                    wait(pe, yev_done[p], CNT[p] * e + max(0, t // 2 - 1))
                    nc.tensor.matmul(pb[4 + t % 4][:, :], hT[:, t * 128:(t + 1) * 128], w2_s[i][:, :],
                                     start=True, stop=True).then_inc(y_done[p], 1)
                pe.wait_ge(y_done[(NT - 1) % 2], CNT[(NT - 1) % 2] * (e + 1))
                pe.sem_inc(w_used[i], 1)
                pe.sem_inc(hT_used, 1)

            def step(j, i, more=True):
                up(j, i)
                if more:
                    transposes(j + i, 1 - i)
                down(j, i)

            transposes(0, 0)
            step(0, 0)
            step(0, 1)
            with pe.Fori(1, PAIRS - 1) as j:
                step(j, 0)
                step(j, 1)
            step(PAIRS - 1, 0)
            step(PAIRS - 1, 1, more=False)

        def copy_tiles(eng, copy, p, j, i):
            e = 2 * j + i
            wait(eng, h_done, 2 * e)
            for n, t in enumerate(range(p, NT, 2)):
                eng.wait_ge(tr_done[p], CNT[p] * e + n + 1)
                copy(xgT[:, :, t * 128:(t + 1) * 128],
                     pb[p][:, :].rearrange("p (c t) -> p c t", c=NC)).then_inc(ev_done[p], 1)

        def weigh_outputs(eng, scaled, p, j, i):
            e = 2 * j + i
            wait(eng, d_to[i], 16 * j + 16)
            wait(eng, d_add[i], 16 * NT * j)
            for n, t in enumerate(range(p, NT, 2)):
                eng.wait_ge(y_done[p], CNT[p] * e + n + 1)
                scaled(yb[i][:, t, :], pb[4 + t % 4][:, :], to_i[i][:, t, 1:2].bitcast(f32)).then_inc(yev_done[p], 1)

        @block.scalar
        def _(act):
            def step(j, i, more=True):
                e = 2 * j + i
                wait(act, g_done, 2 * e)
                for k, (lo, hi) in enumerate(HALF):
                    act.wait_ge(h_done, 2 * e + k + 1)
                    nc.scalar.copy(h3[:, lo:hi], pb[2 + k][F:2 * F, 0:hi - lo]).then_inc(h3_done, 1)
                act.wait_ge(g_done, 2 * e + 2)
                wait(act, hs_done, e)
                nc.scalar.activation(eg[:, :], g13[:, :], ACT.Exp, scale=-1.0).then_inc(e_done, 1)
                if more:
                    copy_tiles(act, nc.scalar.copy, 0, j + i, 1 - i)
                weigh_outputs(act, lambda o, x, w: nc.scalar.activation(o, x, ACT.Copy, scale=w), 0, j, i)

            copy_tiles(act, nc.scalar.copy, 0, 0, 0)
            step(0, 0)
            step(0, 1)
            with act.Fori(1, PAIRS - 1) as j:
                step(j, 0)
                step(j, 1)
            step(PAIRS - 1, 0)
            step(PAIRS - 1, 1, more=False)

        @block.vector
        def _(dve):
            def step(j, i, more=True):
                e = 2 * j + i
                for k, (lo, hi) in enumerate(HALF):
                    dve.wait_ge(h3_done, 2 * e + k + 1)
                    nc.vector.tensor_tensor(g13[:, lo:hi], pb[2 + k][0:F, 0:hi - lo], h3[:, lo:hi],
                                            ALU.mult).then_inc(g_done, 1)
                dve.wait_ge(e_done, e + 1)
                nc.vector.tensor_scalar(eg[:, :], eg[:, :], 1.0, None, ALU.add).then_inc(dn_done, 1)
                dve.wait_ge(dn_done, e + 1)
                nc.vector.reciprocal(eg[:, :], eg[:, :]).then_inc(rc_done, 1)
                dve.wait_ge(rc_done, e + 1)
                wait(dve, hT_used, e)
                nc.vector.tensor_tensor(hT[:, :], g13[:, :], eg[:, :], ALU.mult).then_inc(hs_done, 1)
                if more:
                    copy_tiles(dve, nc.vector.tensor_copy, 1, j + i, 1 - i)
                weigh_outputs(dve, lambda o, x, w: nc.vector.tensor_scalar(o, x, w, None, ALU.mult), 1, j, i)

            copy_tiles(dve, nc.vector.tensor_copy, 1, 0, 0)
            step(0, 0)
            step(0, 1)
            with dve.Fori(1, PAIRS - 1) as j:
                step(j, 0)
                step(j, 1)
            step(PAIRS - 1, 0)
            step(PAIRS - 1, 1, more=False)


def build(nc, x, xT, cT, wq, wk, wv, wo, qw, kw, gateT, w13, w2T, out):
    f32, f32r, bf16, i32, u32 = (mybir.dt.float32, mybir.dt.float32r, mybir.dt.bfloat16,
                                 mybir.dt.int32, mybir.dt.uint32)
    ACT = mybir.ActivationFunctionType
    AX = mybir.AxisListType

    xn2_d = nc.dram_tensor("xn2_scratch", (T, HID), f32, kind="Internal").ap()
    table_d = nc.dram_tensor("token_table", (SPARE + CP, 2), i32, kind="Internal").ap()

    def wait(eng, sem, n, apart=False):
        if isinstance(n, int) and n <= 0:
            return
        if apart:
            wait_apart(eng, (sem, n))
        else:
            eng.wait_ge(sem, n)

    def wait_apart(eng, *pairs):
        with ExitStack() as regs:
            values = []
            for s, n in pairs:
                if not isinstance(n, int):
                    reg = regs.enter_context(eng.register(f"wait_{s.name}_{nc.next_id()}"))
                    eng.reg_add(reg, n, 0)
                    n = reg
                values.append((s, n))
            eng.wait_ge(s_const, 1)
            for s, n in values:
                if not (isinstance(n, int) and n <= 0):
                    eng.wait_ge(s, n)

    keep = ExitStack()
    with keep:
        def sem(name):
            return keep.enter_context(nc.semaphore(name))

        def psum(name):
            return keep.enter_context(nc.psum_tensor(name, [128, 512], f32))

        ident = keep.enter_context(nc.sbuf_tensor("ident", [128, 128], f32))
        ones_b = keep.enter_context(nc.sbuf_tensor("ones_b", [128, 128], bf16))
        macc = keep.enter_context(nc.sbuf_tensor("macc", [128, 2 * E], bf16))
        pb = [psum(f"pb{i}") for i in range(8)]
        s_table, s_const = sem("s_table_scattered"), sem("s_const")

        with ExitStack() as ctx:
            def sb(name, shape, dt=f32):
                return ctx.enter_context(nc.sbuf_tensor(name, shape, dt))

            wqp = [sb(f"wq_{p}", [128, NC, NH * HD], f32r) for p in ("hi", "lo")]
            wkvp = [sb(f"wkv_{p}", [128, 2, NC, NG * HD], f32r) for p in ("hi", "lo")]
            wop = [sb(f"wo_{p}", [128, NH, HID], f32r) for p in ("hi", "lo")]
            xp = [sb(f"x_{p}", [128, NC, 128], f32r) for p in ("hi", "lo")]
            cp = [sb(f"c_{p}", [128, NC, 128], f32r) for p in ("hi", "lo")]
            qp = [sb(f"q_{p}", [128, HPG, 128], f32r) for p in ("hi", "lo")]
            kp = [sb(f"k_{p}", [128, NG, 128], f32r) for p in ("hi", "lo")]
            vp = [sb(f"v_{p}", [128, NG, HD], f32r) for p in ("hi", "lo")]
            ptp = [sb(f"pt_{p}", [128, HPG, 128], f32r) for p in ("hi", "lo")]
            otp = [sb(f"ot_{p}", [128, HPG, 128], f32r) for p in ("hi", "lo")]
            work = sb("work", [128, 8, 512])
            q_nat, probs, k_nat, xn2 = (work[:, i, :] for i in range(4))
            raw, x_stat, x_res = (work[:, i, :] for i in range(4, 7))
            junk = work[:, 7, :].rearrange("p (h t) -> p h t", h=4)
            xn2T = k_nat
            tri = sb("tri", [128, 128], bf16)
            gate = sb("gate", [128, NC, E])
            iota12 = sb("iota12", [128, E])
            mean_w = sb("mean_w", [128, 128])
            sentinel = sb("sentinel", [128, NT, 2], i32)

            small = sb("small", [128, 160])
            at = [0]

            def sm(n, dt=f32):
                v = small[:, at[0]:at[0] + n]
                at[0] += n
                return v if dt is f32 else v.bitcast(dt)

            smax, nmax, psums, rsums = sm(4), sm(4), sm(4), sm(4)
            q_ssq, q_ms, q_rms = sm(4), sm(4), sm(4)
            k_ssq, k_ms, k_rms = sm(4), sm(4), sm(4)
            neghalf = sm(4)
            bn_x, mv_x, eps_x = sm(6), sm(2), sm(1)
            bn_2, mv_2, ve_2, rstd_2 = sm(6), sm(2), sm(1), sm(1)
            wqk, qw_s, kw_s = sm(1), sm(1), sm(1)
            lg, top8, idx8, idxf = sm(E), sm(8), sm(8, u32), sm(2)
            mask = sm(E, bf16)
            posm, pos2, over = sm(2 * E), sm(2), sm(2)
            dst, tokf, entry = sm(2, i32), sm(1), sm(4, i32)
            entry_t = entry.rearrange("p (k o) -> p k o", k=2)
            diff, e10, den = sm(1), sm(1), sm(1)
            list_off = sm(2)

            Q_B, K_B, V_B, S_B, PT_B, QT_B, OT_B, WO_B = pb

            d_w = [sem("d_w_even"), sem("d_w_odd")]
            d_small, d_c, d_x, d_xs, d_xr = sem("d_small"), sem("d_c"), sem("d_x"), sem("d_xs"), sem("d_xr")
            d_x1, d_xn2, d_sent = sem("d_x1_stored"), sem("d_xn2_stored"), sem("d_sentinel")
            s_mw, s_zero = sem("s_mw"), sem("s_zero")
            df_done, e10_done, den_done, w0_done, w1_done = (sem(n) for n in (
                "diff_done", "exp_diff_done", "den10_done", "w0_done", "w1_done"))
            w_mean, w_cent, w_hi, w_lo = sem("w_mean"), sem("w_centred"), sem("w_hi"), sem("w_lo")
            wqk_done = sem("wqk_done")
            c_hi, c_lo, x_hi, x_lo = sem("c_hi"), sem("c_lo"), sem("x_hi"), sem("x_lo")
            k_done, v_done, q_done = sem("k_done"), sem("v_done"), sem("q_done")
            k_cp, k_sq, k_m, k_r, k_sc, k_tr, k_hi, k_lo = (sem(n) for n in (
                "k_copied", "k_squared", "k_meansq", "k_rms", "k_scaled", "k_transposed", "k_hi", "k_lo"))
            v_hi, v_lo = sem("v_hi"), sem("v_lo")
            q_cp, q_sq, q_m, q_r, q_tr, q_hi, q_lo = (sem(n) for n in (
                "q_copied", "q_squared", "q_meansq", "q_rms", "q_transposed", "q_hi", "q_lo"))
            sc_done, mx_done, nm_done, exp_done, rs_done, p_done = (sem(n) for n in (
                "scores_done", "max_done", "negmax_done", "exp_done", "rsum_done", "probs_done"))
            pt_done, pt_hi, pt_lo, ot_done, ot_hi, ot_lo = (sem(n) for n in (
                "pt_done", "pt_hi", "pt_lo", "ot_done", "ot_hi", "ot_lo"))
            wo_used, wo_done, x1_done, b2_done, mv2_done, ve2_done, r2_done, xn2_done = (sem(n) for n in (
                "wo_used", "wo_done", "x1_done", "bn2_done", "mv2_done", "ve2_done", "rstd2_done", "xn2_done"))
            bx_done, mvx_done, eps_done = sem("bnx_done"), sem("mvx_done"), sem("eps_done")
            xt_done, xt_cp, lg_done, lg_cp, t8, i8, ixf, mk = (sem(n) for n in (
                "xn2T_done", "xn2T_copied", "logits_done", "logits_copied", "top8_done", "idx8_done",
                "idxf_done", "mask_done"))
            pos_done, pm, p2, ov, ovb, d0, d1, dst_rdy, tok_i, tok_n, mac = (sem(n) for n in (
                "pos_done", "pos_masked", "pos_reduced", "over_done", "over_big", "dst_a", "dst_b",
                "dst_ready", "token_ids", "token_next", "macc_done"))

            block = ctx.enter_context(nc.Block())

            LOTS = [("k", 0), ("v", 0)] + [("q", n) for n in range(4)] + [("o", n) for n in range(4)]
            NLOT = len(LOTS)
            QLOT = 2

            def lot_parts(l):
                kind, n = LOTS[l]
                if kind == "k":
                    return [w[:, 0, :, :] for w in wkvp]
                if kind == "v":
                    return [w[:, 1, :, :] for w in wkvp]
                if kind == "q":
                    return [w[:, :, n * 512:(n + 1) * 512] for w in wqp]
                return [w[:, 4 * n:4 * n + 4, :] for w in wop]

            def stage(l):
                return work[:, 4 * (l % 2):4 * (l % 2) + 4, :]

            @block.sync
            def _(sp):
                sp.dma_start(gate[:, :, :], gateT).then_inc(d_small, 16)
                sp.dma_start(qw_s, qw).then_inc(d_small, 16)
                sp.dma_start(kw_s, kw).then_inc(d_small, 16)
                for l, (kind, n) in enumerate(LOTS):
                    if l >= 2:
                        sp.wait_ge(w_lo, l - 1)
                    if kind in "kv":
                        src = (wk if kind == "k" else wv).rearrange("(c p) n -> p c n", p=128)
                    elif kind == "q":
                        src = wq.rearrange("(c p) n -> p c n", p=128)[:, :, n * 512:(n + 1) * 512]
                    else:
                        src = wo.rearrange("(h p) n -> p h n", p=128)[:, 4 * n:4 * n + 4, :]
                    sp.dma_start(stage(l), src).then_inc(d_w[l % 2], 16)
                sp.wait_ge(s_const, 1)
                sp.dma_start(table_d[LIST1:, :].rearrange("(e p t) o -> p e (t o)", p=128, t=NT),
                             sentinel[:, :, :].rearrange("p t o -> p (t o)")[:, None, :].broadcast_to(
                                 [128, E + 1, 2 * NT])).then_inc(d_sent, 16)
                sp.dma_start(out[T:T + CP, :], x.rearrange("b t n -> (b t) n")[0:CP, :]).then_inc(d_sent, 16)
                sp.wait_ge(w_lo, NLOT)

                raw_v = raw.rearrange("p (c t) -> p c t", c=NC)

                def load_c(b):
                    wait(sp, x_lo, b)
                    sp.dma_start(raw_v, cT[b]).then_inc(d_c, 16)

                def load_x(b):
                    wait(sp, c_lo, b + 1)
                    sp.dma_start(raw_v, xT[b]).then_inc(d_x, 16)

                def load_stat(b):
                    wait(sp, bx_done, b)
                    sp.dma_start(x_stat, x[b]).then_inc(d_xs, 16)

                def load_res(b):
                    wait_apart(sp, (xn2_done, b), (d_x1, 16 * b))
                    sp.dma_start(x_res, x[b]).then_inc(d_xr, 16)

                def store_x1(b):
                    wait(sp, x1_done, b + 1)
                    sp.dma_start(out[bass.ds(b * 128, 128), :], x_res).then_inc(d_x1, 16)

                def store_xn2(b):
                    wait_apart(sp, (xn2_done, b + 1))
                    sp.dma_start(xn2_d[bass.ds(b * 128, 128), :], xn2).then_inc(d_xn2, 16)

                load_c(0)
                load_stat(0)
                load_x(0)
                load_res(0)

                def body(b, first=False, last=False):
                    if not last:
                        load_c(b + 1)
                        load_stat(b + 1)
                    if not first:
                        store_x1(b - 1)
                    if not last:
                        load_x(b + 1)
                    if not first:
                        store_xn2(b - 1)
                        load_res(b)

                body(0, first=True)
                body(1)
                with sp.Fori(2, NB - 1) as b:
                    body(b)
                body(NB - 1, last=True)
                store_x1(NB - 1)
                store_xn2(NB - 1)
                sp.wait_ge(d_x1, 16 * NB)
                sp.wait_ge(d_xn2, 16 * NB)
                sp.wait_ge(d_sent, 32)

            @block.tensor
            def _(pe):
                pe.wait_ge(s_mw, 1)
                for n in range(4):
                    l = QLOT + n
                    pe.wait_ge(d_w[l % 2], 16 * (l // 2 + 1))
                    for c in range(NC):
                        last_mm = nc.tensor.matmul(pb[n][:, :], mean_w[:, :], stage(l)[:, c, :],
                                                   start=(c == 0), stop=(c == NC - 1))
                    last_mm.then_inc(w_mean, 1)

                PARTS = ((0, 0), (0, 1), (1, 0))

                def project(bank, lhs, rhs):
                    n = 0
                    for c in range(NC):
                        for a, b_ in PARTS:
                            mm = nc.tensor.matmul(bank[:, :], lhs[a][:, c, :], rhs[b_][:, c, :],
                                                  start=(n == 0), stop=(n == 3 * NC - 1))
                            n += 1
                    return mm

                def keys(b):
                    wait(pe, c_lo, b + 1)
                    wait(pe, lg_cp, b - 1)
                    wait(pe, k_lo, b)
                    project(K_B, cp, [w[:, 0, :, :] for w in wkvp]).then_inc(k_done, 1)

                def values(b):
                    wait(pe, v_lo, b)
                    project(V_B, cp, [w[:, 1, :, :] for w in wkvp]).then_inc(v_done, 1)

                def queries(b, g):
                    if g == 0:
                        wait(pe, x_lo, b + 1)
                    wait(pe, q_cp, 4 * b + g)
                    project(Q_B, xp, [w[:, :, g * 512:(g + 1) * 512] for w in wqp]).then_inc(q_done, 1)

                def transpose_q(b, g):
                    u = 4 * b + g
                    wait(pe, q_cp, u + 1)
                    wait(pe, q_lo, u)
                    for h in range(HPG):
                        tr = nc.tensor.transpose(QT_B[:, h * 128:(h + 1) * 128],
                                                 q_nat[:, h * 128:(h + 1) * 128], ident[:, :])
                    tr.then_inc(q_tr, 1)

                def transpose_k(b):
                    wait(pe, k_sc, b + 1)
                    for g in range(NG):
                        tr = nc.tensor.transpose(K_B[:, g * 128:(g + 1) * 128],
                                                 k_nat[:, g * 128:(g + 1) * 128], ident[:, :])
                    tr.then_inc(k_tr, 1)

                def scores(b, g):
                    u = 4 * b + g
                    if g == 0:
                        wait(pe, k_lo, b + 1)
                    wait(pe, q_lo, u + 1)
                    wait(pe, exp_done, u)
                    for h in range(HPG):
                        for n, (a, b_) in enumerate(PARTS):
                            mm = nc.tensor.matmul(S_B[:, h * 128:(h + 1) * 128], qp[a][:, h, :],
                                                  kp[b_][:, g, :], start=(n == 0), stop=(n == 2))
                    mm.then_inc(sc_done, 1)

                def transpose_p(b, g):
                    u = 4 * b + g
                    wait(pe, p_done, u + 1)
                    wait(pe, pt_lo, u)
                    for h in range(HPG):
                        tr = nc.tensor.transpose(PT_B[:, h * 128:(h + 1) * 128],
                                                 probs[:, h * 128:(h + 1) * 128], ident[:, :])
                    tr.then_inc(pt_done, 1)

                def attend(b, g):
                    u = 4 * b + g
                    wait(pe, v_lo, b + 1)
                    wait(pe, pt_lo, u + 1)
                    wait(pe, ot_lo, u)
                    if g == 3:
                        wait(pe, pos_read_count, b)
                    for n, (a, b_) in enumerate(PARTS):
                        mm = nc.tensor.matmul(OT_B[:, :], vp[a][:, g, :], ptp[b_][:, :, :],
                                              start=(n == 0), stop=(n == 2))
                    mm.then_inc(ot_done, 1)

                def out_project(b, g, half):
                    u = 4 * b + g
                    if half == 0:
                        wait(pe, ot_lo, u + 1)
                        if g == 0:
                            wait(pe, x1_done, b)
                    for h in (2 * half, 2 * half + 1):
                        for n, (a, b_) in enumerate(PARTS):
                            mm = nc.tensor.matmul(WO_B[:, :], otp[a][:, h, :], wop[b_][:, g * HPG + h, :],
                                                  start=(g == 0 and h == 0 and n == 0),
                                                  stop=(g == NG - 1 and h == HPG - 1 and n == 2))
                    if half == 1:
                        mm.then_inc(wo_used, 1)

                def transpose_x(b):
                    wait(pe, xn2_done, b + 1)
                    wait(pe, k_lo, b + 2)
                    for c in range(NC):
                        tr = nc.tensor.transpose(K_B[:, c * 128:(c + 1) * 128],
                                                 xn2[:, c * 128:(c + 1) * 128], ident[:, :])
                    tr.then_inc(xt_done, 1)

                def route(b):
                    wait(pe, xt_cp, b + 1)
                    for c in range(NC):
                        mm = nc.tensor.matmul(K_B[:, 0:E], xn2T[:, c * 128:(c + 1) * 128], gate[:, c, :],
                                              start=(c == 0), stop=(c == NC - 1))
                    mm.then_inc(lg_done, 1)

                def positions(b):
                    wait(pe, mk, b + 1)
                    wait(pe, mac, b + 1)
                    wait(pe, ot_lo, 4 * b + 7)
                    nc.tensor.matmul(OT_B[:, 0:2 * E], tri[:, :], mask, start=True, stop=False)
                    nc.tensor.matmul(OT_B[:, 0:2 * E], ones_b[:, :], macc[:, :],
                                     start=False, stop=True).then_inc(pos_done, 1)

                pos_read_count = pm
                pe.wait_ge(s_const, 1)
                pe.wait_ge(d_small, 48)
                pe.wait_ge(w_lo, NLOT)
                keys(0)
                values(0)
                queries(0, 0)
                transpose_k(0)
                transpose_q(0, 0)

                def body(b, first=False, last=False):
                    for g in range(NG):
                        has_prev = not (first and g == 0)
                        has_next = not (last and g == NG - 1)
                        prev = (b, g - 1) if g else (b - 1, NG - 1)
                        nxt = (b, g + 1) if g < NG - 1 else (b + 1, 0)
                        scores(b, g)
                        if has_prev:
                            attend(*prev)
                        if g == 3 and not last:
                            keys(b + 1)
                            values(b + 1)
                        if has_next:
                            queries(*nxt)
                        if g == 2 and not first:
                            transpose_x(b - 1)
                        if has_prev:
                            out_project(*prev, 0)
                        if has_next:
                            transpose_q(*nxt)
                        transpose_p(b, g)
                        if g == 3 and not last:
                            transpose_k(b + 1)
                        if g == 2 and not first:
                            route(b - 1)
                        if g == 3 and not first:
                            positions(b - 1)
                        if has_prev:
                            out_project(*prev, 1)

                body(0, first=True)
                body(1)
                with pe.Fori(2, NB - 1) as b:
                    body(b)
                body(NB - 1, last=True)
                attend(NB - 1, NG - 1)
                out_project(NB - 1, NG - 1, 0)
                out_project(NB - 1, NG - 1, 1)
                pe.wait_ge(xn2_done, NB)
                for c in range(NC):
                    tr = nc.tensor.transpose(K_B[:, c * 128:(c + 1) * 128],
                                             xn2[:, c * 128:(c + 1) * 128], ident[:, :])
                tr.then_inc(xt_done, 1)
                route(NB - 1)
                pe.wait_ge(mk, NB)
                pe.wait_ge(mac, NB)
                pe.wait_ge(ot_lo, NU)
                nc.tensor.matmul(OT_B[:, 0:2 * E], tri[:, :], mask, start=True, stop=False)
                nc.tensor.matmul(OT_B[:, 0:2 * E], ones_b[:, :], macc[:, :],
                                 start=False, stop=True).then_inc(pos_done, 1)

            @block.scalar
            def _(act):
                for l, (kind, n) in enumerate(LOTS):
                    if kind == "q":
                        act.wait_ge(w_cent, l - QLOT + 1)
                    else:
                        act.wait_ge(d_w[l % 2], 16 * (l // 2 + 1))
                    nc.scalar.copy(lot_parts(l)[0], stage(l)).then_inc(w_hi, 1)

                raw_v = raw.rearrange("p (c t) -> p c t", c=NC)

                def split_c(b):
                    wait(act, d_c, 16 * (b + 1))
                    wait(act, v_done, b)
                    nc.scalar.copy(cp[0][:, :, :], raw_v).then_inc(c_hi, 1)

                def split_x(b):
                    wait(act, d_x, 16 * (b + 1))
                    wait(act, q_done, 4 * b)
                    nc.scalar.copy(xp[0][:, :, :], raw_v).then_inc(x_hi, 1)

                def copy_k(b):
                    wait(act, k_done, b + 1)
                    wait(act, k_tr, b)
                    wait(act, lg_done, b - 1)
                    nc.scalar.copy(k_nat, K_B[:, :]).then_inc(k_cp, 1)

                def split_k(b):
                    wait(act, k_tr, b + 1)
                    wait(act, sc_done, 4 * b)
                    if isinstance(b, int) and b == 0:
                        act.wait_ge(wqk_done, 1)
                    nc.scalar.activation(kp[0][:, :, :], K_B[:, :].rearrange("p (g t) -> p g t", g=NG),
                                         ACT.Copy, scale=wqk).then_inc(k_hi, 1)

                def split_v(b):
                    wait(act, v_done, b + 1)
                    wait(act, ot_done, 4 * b)
                    nc.scalar.copy(vp[0][:, :, :], V_B[:, :].rearrange("p (g t) -> p g t", g=NG)).then_inc(v_hi, 1)

                def copy_q(b, g):
                    u = 4 * b + g
                    wait(act, q_done, u + 1)
                    wait(act, q_tr, u)
                    wait(act, q_sq, u)
                    nc.scalar.copy(q_nat, Q_B[:, :]).then_inc(q_cp, 1)

                def split_q(b, g):
                    u = 4 * b + g
                    wait(act, q_tr, u + 1)
                    wait(act, sc_done, u)
                    nc.scalar.copy(qp[0][:, :, :], QT_B[:, :].rearrange("p (h t) -> p h t", h=HPG)).then_inc(q_hi, 1)

                def exps(b, g):
                    u = 4 * b + g
                    wait(act, nm_done, u + 1)
                    wait(act, pt_done, u)
                    for h in range(HPG):
                        ex = nc.scalar.activation(probs[:, h * 128:(h + 1) * 128], S_B[:, h * 128:(h + 1) * 128],
                                                  ACT.Exp, bias=nmax[:, h:h + 1], scale=q_rms[:, h:h + 1],
                                                  accum_out=psums[:, h:h + 1])
                    ex.then_inc(exp_done, 1)

                def split_p(b, g):
                    u = 4 * b + g
                    wait(act, pt_done, u + 1)
                    wait(act, ot_done, u)
                    nc.scalar.copy(ptp[0][:, :, :], PT_B[:, :].rearrange("p (h t) -> p h t", h=HPG)).then_inc(pt_hi, 1)

                def split_o(b, g):
                    u = 4 * b + g
                    wait(act, ot_done, u + 1)
                    wait(act, wo_used, u)
                    nc.scalar.copy(otp[0][:, :, :], OT_B[:, :].rearrange("p (h t) -> p h t", h=HPG)).then_inc(ot_hi, 1)

                def exp_diff(b):
                    wait(act, df_done, b + 1)
                    wait(act, w1_done, b)
                    nc.scalar.activation(e10, diff, ACT.Exp).then_inc(e10_done, 1)

                def copy_xt(b, keys_after=True):
                    wait(act, xt_done, b + 1)
                    if keys_after:
                        wait(act, k_tr, b + 2)
                    nc.scalar.copy(xn2T, K_B[:, :]).then_inc(xt_cp, 1)

                act.wait_ge(w_lo, NLOT)
                split_c(0)
                split_x(0)
                copy_k(0)
                copy_q(0, 0)
                split_k(0)
                split_q(0, 0)

                def body(b, first=False, last=False):
                    for g in range(NG):
                        prev = (b, g - 1) if g else (b - 1, NG - 1)
                        nxt = (b, g + 1) if g < NG - 1 else (b + 1, 0)
                        if not (first and g == 0):
                            split_o(*prev)
                        if g == 0:
                            split_v(b)
                        exps(b, g)
                        if g == 1 and not last:
                            split_c(b + 1)
                        if g == 3 and not last:
                            split_x(b + 1)
                            copy_k(b + 1)
                        if not (last and g == NG - 1):
                            copy_q(*nxt)
                        if g == 2 and not first:
                            copy_xt(b - 1)
                        if g == 3 and not first:
                            exp_diff(b - 1)
                        if not (last and g == NG - 1):
                            split_q(*nxt)
                        split_p(b, g)
                        if g == 3 and not last:
                            split_k(b + 1)

                body(0, first=True)
                body(1)
                with act.Fori(2, NB - 1) as b:
                    body(b)
                body(NB - 1, last=True)
                split_o(NB - 1, NG - 1)
                copy_xt(NB - 1, keys_after=False)
                exp_diff(NB - 1)

            @block.vector
            def _(dve):
                def minus(part, whole):
                    return nc.vector.tensor_tensor(part[1], whole, part[0].bitcast(f32), ALU.subtract)

                nc.vector.memset(mean_w[:, :], 1.0 / HID).then_inc(s_mw, 1)
                nc.vector.memset(neghalf, -0.5)
                nc.vector.memset(macc[:, :], 0.0)
                nc.vector.memset(list_off[:, 0:1], 0.0)
                nc.vector.memset(list_off[:, 1:2], float(LIST1)).then_inc(mac, 1)
                dve.wait_ge(d_small, 48)
                nc.vector.tensor_tensor(wqk, qw_s, kw_s, ALU.mult).then_inc(wqk_done, 1)
                for l, (kind, n) in enumerate(LOTS):
                    if kind == "q":
                        dve.wait_ge(w_mean, n + 1)
                        nc.vector.tensor_tensor(stage(l), stage(l),
                                                pb[n][:, None, :].broadcast_to([128, NC, 512]),
                                                ALU.subtract).then_inc(w_cent, 1)
                    dve.wait_ge(w_hi, l + 1)
                    hi, lo = lot_parts(l)
                    nc.vector.tensor_tensor(lo, stage(l), hi.bitcast(f32), ALU.subtract).then_inc(w_lo, 1)

                raw_v = raw.rearrange("p (c t) -> p c t", c=NC)

                def view(bank, n=4):
                    return bank[:, :].rearrange("p (h t) -> p h t", h=n)

                def all3(parts):
                    return [p[:, :, :] for p in parts]

                def split_c(b):
                    wait(dve, c_hi, b + 1)
                    minus(all3(cp), raw_v).then_inc(c_lo, 1)

                def split_x(b):
                    wait(dve, x_hi, b + 1)
                    minus(all3(xp), raw_v).then_inc(x_lo, 1)

                def stats_x(b):
                    wait(dve, d_xs, 16 * (b + 1))
                    wait(dve, mvx_done, b)
                    nc.vector.bn_stats(bn_x, x_stat).then_inc(bx_done, 1)
                    wait(dve, bx_done, b + 1, apart=True)
                    wait(dve, eps_done, b)
                    nc.vector.bn_aggr(mv_x, bn_x).then_inc(mvx_done, 1)

                def square_k(b):
                    wait(dve, k_cp, b + 1)
                    wait(dve, k_m, b)
                    wait(dve, q_sq, 4 * b)
                    for g in range(NG):
                        kk = k_nat[:, g * 128:(g + 1) * 128]
                        sq = nc.vector.tensor_tensor_reduce(out=junk[:, g, :], in0=kk, in1=kk, scale=1.0, scalar=0.0,
                                                            op0=ALU.mult, op1=ALU.add, accum_out=k_ssq[:, g:g + 1])
                    sq.then_inc(k_sq, 1)

                def scale_k(b):
                    wait(dve, k_r, b + 1)
                    kv = k_nat.rearrange("p (g t) -> p g t", g=NG)
                    nc.vector.tensor_tensor(kv, kv, k_rms[:, :, None].broadcast_to([128, NG, 128]),
                                            ALU.mult).then_inc(k_sc, 1)

                def split_k(b):
                    wait(dve, k_hi, b + 1)
                    nc.vector.scalar_tensor_tensor(out=kp[1][:, :, :], in0=view(K_B), scalar=wqk,
                                                   in1=kp[0][:, :, :].bitcast(f32), op0=ALU.mult,
                                                   op1=ALU.subtract).then_inc(k_lo, 1)

                def split_v(b):
                    wait(dve, v_hi, b + 1)
                    minus(all3(vp), view(V_B)).then_inc(v_lo, 1)

                def square_q(b, g):
                    u = 4 * b + g
                    wait(dve, q_cp, u + 1)
                    wait(dve, q_m, u)
                    if g == 0:
                        wait(dve, k_sq, b + 1)
                    for h in range(HPG):
                        qq = q_nat[:, h * 128:(h + 1) * 128]
                        sq = nc.vector.tensor_tensor_reduce(out=junk[:, h, :], in0=qq, in1=qq, scale=1.0, scalar=0.0,
                                                            op0=ALU.mult, op1=ALU.add, accum_out=q_ssq[:, h:h + 1])
                    sq.then_inc(q_sq, 1)

                def split_q(b, g):
                    wait(dve, q_hi, 4 * b + g + 1)
                    minus(all3(qp), view(QT_B)).then_inc(q_lo, 1)

                def maxima(b, g):
                    u = 4 * b + g
                    wait(dve, sc_done, u + 1)
                    nc.vector.tensor_reduce(smax, view(S_B), AX.X, ALU.max).then_inc(mx_done, 1)
                    wait(dve, mx_done, u + 1)
                    wait(dve, q_r, u + 1)
                    wait(dve, exp_done, u)
                    nc.vector.scalar_tensor_tensor(out=nmax, in0=smax, scalar=-1.0, in1=q_rms,
                                                   op0=ALU.mult, op1=ALU.mult).then_inc(nm_done, 1)

                def normalise(b, g):
                    u = 4 * b + g
                    wait(dve, exp_done, u + 1)
                    wait(dve, p_done, u)
                    nc.vector.reciprocal(rsums, psums).then_inc(rs_done, 1)
                    wait(dve, rs_done, u + 1)
                    pv = probs.rearrange("p (h t) -> p h t", h=HPG)
                    nc.vector.tensor_tensor(pv, pv, rsums[:, :, None].broadcast_to([128, HPG, 128]),
                                            ALU.mult).then_inc(p_done, 1)

                def split_p(b, g):
                    wait(dve, pt_hi, 4 * b + g + 1)
                    minus(all3(ptp), view(PT_B)).then_inc(pt_lo, 1)

                def split_o(b, g):
                    wait(dve, ot_hi, 4 * b + g + 1)
                    minus(all3(otp), view(OT_B)).then_inc(ot_lo, 1)

                def residual(b):
                    wait(dve, wo_used, 4 * b + 4)
                    wait(dve, d_xr, 16 * (b + 1))
                    nc.vector.tensor_tensor(x_res, x_res, WO_B[:, :], ALU.add).then_inc(x1_done, 1)

                def stats_2(b):
                    wait(dve, x1_done, b + 1)
                    nc.vector.bn_stats(bn_2, x_res).then_inc(b2_done, 1)
                    wait(dve, b2_done, b + 1, apart=True)
                    wait(dve, ve2_done, b)
                    wait(dve, xn2_done, b)
                    nc.vector.bn_aggr(mv_2, bn_2).then_inc(mv2_done, 1)

                def norm2(b):
                    wait(dve, r2_done, b + 1)
                    wait(dve, d_xn2, 16 * b)
                    wait(dve, xt_done, b)
                    nc.vector.tensor_scalar(xn2, x_res, mv_2[:, 0:1], rstd_2, ALU.subtract,
                                            ALU.mult).then_inc(xn2_done, 1)

                def copy_logits(b):
                    wait(dve, lg_done, b + 1)
                    nc.vector.tensor_copy(lg, K_B[:, 0:E]).then_inc(lg_cp, 1)

                def choose(b):
                    wait(dve, lg_cp, b + 1, apart=True)
                    nc.vector.max(top8, lg).then_inc(t8, 1)
                    wait(dve, t8, b + 1, apart=True)
                    nc.vector.max_index(idx8, top8, lg).then_inc(i8, 1)
                    wait(dve, i8, b + 1)
                    nc.vector.tensor_copy(idxf, idx8[:, 0:2]).then_inc(ixf, 1)
                    nc.vector.tensor_tensor(diff, top8[:, 1:2], top8[:, 0:1], ALU.subtract).then_inc(df_done, 1)
                    wait(dve, ixf, b + 1)
                    wait(dve, pos_done, b)
                    nc.vector.tensor_tensor(mask.rearrange("p (k e) -> p k e", k=2),
                                            iota12[:, None, :].broadcast_to([128, 2, E]),
                                            idxf[:, :, None].broadcast_to([128, 2, E]),
                                            ALU.is_equal).then_inc(mk, 1)

                def place(b):
                    wait(dve, pos_done, b + 1)
                    nc.vector.tensor_tensor(posm, OT_B[:, 0:2 * E], mask, ALU.mult).then_inc(pm, 1)
                    wait(dve, mac, b + 1)
                    nc.vector.tensor_tensor(macc[:, :], macc[:, :], mask, ALU.add).then_inc(mac, 1)
                    wait(dve, e10_done, b + 1)
                    nc.vector.tensor_scalar(den, e10, 1.0, None, ALU.add).then_inc(den_done, 1)
                    wait(dve, pm, b + 1)
                    nc.vector.tensor_reduce(pos2, posm.rearrange("p (k e) -> p k e", k=2), AX.X,
                                            ALU.add).then_inc(p2, 1)
                    wait(dve, den_done, b + 1)
                    wait(dve, s_table, 32 * b)
                    nc.vector.reciprocal(entry_t[:, 0, 1:2].bitcast(f32), den).then_inc(w0_done, 1)
                    wait(dve, p2, b + 1)
                    nc.vector.tensor_scalar(over, pos2, float(CAP), float(BIG), ALU.is_ge, ALU.mult).then_inc(ov, 1)
                    wait(dve, w0_done, b + 1)
                    nc.vector.tensor_tensor(entry_t[:, 1, 1:2].bitcast(f32), entry_t[:, 0, 1:2].bitcast(f32), e10,
                                            ALU.mult).then_inc(w1_done, 1)
                    wait(dve, ov, b + 1)
                    nc.vector.tensor_tensor(over, over, pos2, ALU.add).then_inc(ovb, 1)
                    wait(dve, tok_n, b)
                    nc.vector.tensor_copy(entry_t[:, :, 0], tokf.broadcast_to([128, 2])).then_inc(tok_i, 1)
                    wait(dve, ovb, b + 1)
                    nc.vector.scalar_tensor_tensor(out=over[:, 0:1], in0=idxf[:, 0:1], scalar=float(STRIDE),
                                                   in1=over[:, 0:1], op0=ALU.mult, op1=ALU.add)
                    nc.vector.scalar_tensor_tensor(out=over[:, 1:2], in0=idxf[:, 1:2], scalar=float(CP),
                                                   in1=over[:, 1:2], op0=ALU.mult, op1=ALU.add).then_inc(d0, 1)
                    wait(dve, tok_i, b + 1)
                    nc.vector.tensor_scalar(tokf, tokf, 128.0, None, ALU.add).then_inc(tok_n, 1)
                    wait(dve, d0, b + 1)
                    nc.vector.tensor_tensor(dst, over, list_off, ALU.add).then_inc(dst_rdy, 1)

                dve.wait_ge(s_const, 1)
                split_c(0)
                split_x(0)
                stats_x(0)
                square_k(0)
                square_q(0, 0)
                scale_k(0)
                split_k(0)
                split_q(0, 0)

                def body(b, first=False, last=False):
                    for g in range(NG):
                        prev = (b, g - 1) if g else (b - 1, NG - 1)
                        nxt = (b, g + 1) if g < NG - 1 else (b + 1, 0)
                        if g == 1 and not first:
                            residual(b - 1)
                        if g == 3 and not first:
                            copy_logits(b - 1)
                        maxima(b, g)
                        if not (first and g == 0):
                            split_o(*prev)
                        if g == 0:
                            split_v(b)
                        if g == 2 and not first:
                            norm2(b - 1)
                        if g == 3 and not first:
                            choose(b - 1)
                        normalise(b, g)
                        if g == 1 and not first:
                            stats_2(b - 1)
                        if g == 1 and not last:
                            split_c(b + 1)
                        if g == 3 and not last:
                            split_x(b + 1)
                            stats_x(b + 1)
                            square_k(b + 1)
                        if not (last and g == NG - 1):
                            square_q(*nxt)
                        if g == 3 and not last:
                            scale_k(b + 1)
                        if not (last and g == NG - 1):
                            split_q(*nxt)
                        split_p(b, g)
                        if g == 3 and not last:
                            split_k(b + 1)
                        if g == 3 and not first:
                            place(b - 1)

                body(0, first=True)
                body(1)
                with dve.Fori(2, NB - 1) as b:
                    body(b)
                body(NB - 1, last=True)
                split_o(NB - 1, NG - 1)
                residual(NB - 1)
                stats_2(NB - 1)
                norm2(NB - 1)
                copy_logits(NB - 1)
                choose(NB - 1)
                place(NB - 1)

            @block.gpsimd
            def _(pool):
                nc.gpsimd.memset(ident[:, :], 0.0)
                nc.gpsimd.memset(ones_b[:, :], 1.0)
                nc.gpsimd.memset(tri[:, :], 1.0)
                nc.gpsimd.iota(iota12[:, :], pattern=[[1, E]], base=0, channel_multiplier=0,
                               allow_small_or_imprecise_dtypes=True)
                nc.gpsimd.iota(tokf, pattern=[[0, 1]], base=0, channel_multiplier=1,
                               allow_small_or_imprecise_dtypes=True)
                nc.gpsimd.memset(sentinel[:, :, 1], 0)
                nc.gpsimd.iota(sentinel[:, :, 0], pattern=[[1, NT]], base=T,
                               channel_multiplier=NT).then_inc(s_zero, 1)
                pool.wait_ge(s_zero, 1)
                nc.gpsimd.affine_select(out=ident[:, :], in_=ident[:, :], compare_op=ALU.not_equal, fill=1.0,
                                        base=0, pattern=[[-1, 128]], channel_multiplier=1)
                nc.gpsimd.affine_select(out=tri[:, :], in_=tri[:, :], compare_op=ALU.is_gt, fill=0.0,
                                        base=0, pattern=[[1, 128]], channel_multiplier=-1).then_inc(s_const, 1)

                def eps_of_x(b):
                    wait(pool, mvx_done, b + 1, apart=True)
                    nc.gpsimd.tensor_scalar(eps_x, mv_x[:, 1:2], HD * ATTN_EPS, HD * ATTN_EPS * LN_EPS,
                                            ALU.mult, ALU.add).then_inc(eps_done, 1)

                def rms_k(b):
                    wait(pool, k_sq, b + 1, apart=True)
                    nc.gpsimd.tensor_scalar(k_ms, k_ssq, 1.0 / HD, ATTN_EPS, ALU.mult, ALU.add).then_inc(k_m, 1)
                    wait(pool, k_m, b + 1)
                    wait(pool, k_sc, b)
                    nc.gpsimd.tensor_tensor(k_rms, k_ms, neghalf, ALU.pow).then_inc(k_r, 1)

                def rms_q(b, g):
                    u = 4 * b + g
                    wait(pool, q_sq, u + 1)
                    if g == 0:
                        wait(pool, eps_done, b + 1)
                    nc.gpsimd.tensor_tensor(q_ms, q_ssq, eps_x.broadcast_to([128, HPG]), ALU.add).then_inc(q_m, 1)
                    wait(pool, q_m, u + 1)
                    wait(pool, exp_done, u)
                    nc.gpsimd.tensor_tensor(q_rms, q_ms, neghalf, ALU.pow).then_inc(q_r, 1)

                def rstd2(b):
                    wait(pool, mv2_done, b + 1, apart=True)
                    nc.gpsimd.tensor_scalar(ve_2, mv_2[:, 1:2], LN_EPS, None, ALU.add).then_inc(ve2_done, 1)
                    wait(pool, ve2_done, b + 1)
                    wait(pool, xn2_done, b)
                    nc.gpsimd.tensor_tensor(rstd_2, ve_2, neghalf[:, 0:1], ALU.pow).then_inc(r2_done, 1)

                def scatter(b):
                    wait_apart(pool, (dst_rdy, b + 1), (w1_done, b + 1))
                    for k in range(2):
                        nc.gpsimd.indirect_dma_start(
                            out=table_d, out_offset=bass.IndirectOffsetOnAxis(ap=dst[:, k:k + 1], axis=0),
                            in_=entry_t[:, k, :], in_offset=None, bounds_check=SPARE - 1,
                            oob_is_err=False).then_inc(s_table, 16)

                pool.wait_ge(mac, 1)
                pool.wait_ge(d_sent, 32)
                eps_of_x(0)
                rms_k(0)
                rms_q(0, 0)

                def body(b, first=False, last=False):
                    for g in range(NG):
                        nxt = (b, g + 1) if g < NG - 1 else (b + 1, 0)
                        if g == 3 and not last:
                            eps_of_x(b + 1)
                            rms_k(b + 1)
                        if g == 1 and not first:
                            rstd2(b - 1)
                        if not (last and g == NG - 1):
                            rms_q(*nxt)
                        if g == 3 and not first:
                            scatter(b - 1)

                body(0, first=True)
                body(1)
                with pool.Fori(2, NB - 1) as b:
                    body(b)
                body(NB - 1, last=True)
                rstd2(NB - 1)
                scatter(NB - 1)
                pool.wait_ge(s_table, 32 * NB)

        experts(nc, gt=dict(wait=wait, wait_apart=wait_apart, sem=sem, pb=pb, ident=ident, ones_b=ones_b,
                            macc=macc, xn2_d=xn2_d, table_d=table_d), w13=w13, w2T=w2T, out=out)
    return nc


def kernel(x, ctx_2048, L0_xattn_Wq, L0_xattn_Wk, L0_xattn_Wv, L0_xattn_Wo, L0_xattn_q_norm_w,
           L0_xattn_k_norm_w, L0_ffn_gate_w, L0_ffn_w1, L0_ffn_w2, L0_ffn_w3):
    import concourse.bacc as bacc
    from concourse.bass_utils import run_bass_kernel_spmd

    def by_width(a):
        a = np.asarray(a)
        return np.ascontiguousarray(a.reshape(NB, SEQ, NC, 128).transpose(0, 3, 2, 1))

    def pieces(a):
        return np.ascontiguousarray(a.reshape(NC, 128, -1).transpose(1, 0, 2))

    w1, w2, w3 = (np.asarray(a) for a in (L0_ffn_w1, L0_ffn_w2, L0_ffn_w3))
    w13 = np.concatenate([w1, w3], axis=1).transpose(0, 2, 1)
    w13 = np.ascontiguousarray(w13.reshape(E, NC, 128, 2 * F).transpose(0, 2, 1, 3))
    arrays = {
        "x": np.ascontiguousarray(x), "xT": by_width(x), "cT": by_width(ctx_2048),
        "wq": np.ascontiguousarray(L0_xattn_Wq), "wk": np.ascontiguousarray(L0_xattn_Wk),
        "wv": np.ascontiguousarray(L0_xattn_Wv), "wo": np.ascontiguousarray(L0_xattn_Wo),
        "qw": np.asarray(L0_xattn_q_norm_w).reshape(HD, 1), "kw": np.asarray(L0_xattn_k_norm_w).reshape(HD, 1),
        "gateT": pieces(np.asarray(L0_ffn_gate_w).T), "w13": w13,
        "w2T": np.ascontiguousarray(w2.transpose(0, 2, 1)),
    }
    nc = bacc.Bacc("TRN2", target_bir_lowering=False, num_devices=1)
    aps = {n: nc.dram_tensor(n, a.shape, mybir.dt.from_np(a.dtype), kind="ExternalInput").ap()
           for n, a in arrays.items()}
    out = nc.dram_tensor("out", (T + CP, HID), mybir.dt.float32, kind="ExternalOutput").ap()
    build(nc, out=out, **aps)
    result = run_bass_kernel_spmd(nc, [arrays], core_ids=[0])
    return result.results[0]["out"][:T].reshape(NB, SEQ, HID)
```

```python
from contextlib import ExitStack

import numpy as np

import concourse.bass as bass
from concourse import mybir
from concourse.alu_op_type import AluOpType as ALU

NB, SEQ, HID = 64, 128, 512
NH, NG, HD = 16, 4, 128
HPG = NH // NG
NC = HID // 128
NU = NB * NG
T = NB * SEQ
E, F = 12, 64
CAP = -(-T * 5 // (4 * E))
NT = -(-CAP // 128)
assert CAP % NT == 0
CP = NT * 128
STRIDE = 2 * CP
LIST1 = E * STRIDE
ROWS = LIST1 + E * CP
BIG = 1 << 20
ATTN_EPS, LN_EPS = 1e-6, 1e-5
LOWEST = float(np.finfo(np.float32).min)


def experts(nc, gt, w13, w2T, out):
    f32, f32r, i32 = mybir.dt.float32, mybir.dt.float32r, mybir.dt.int32
    ACT = mybir.ActivationFunctionType
    wait, wait_apart, sem, pb, ident, ones_b, macc, xn2_d, table_d = (gt[k] for k in (
        "wait", "wait_apart", "sem", "pb", "ident", "ones_b", "macc", "xn2_d", "table_d"))

    with ExitStack() as ctx:
        def sb(name, shape, dt=f32):
            return ctx.enter_context(nc.sbuf_tensor(name, shape, dt))

        tot, first_n = sb("tot", [128, E]), sb("first_n", [128, E], i32)
        w13_s = [sb(f"w13_{i}", [128, NC, 2 * F]) for i in range(2)]
        w2_s = [sb(f"w2_{i}", [2 * F, HID]) for i in range(2)]
        w2_hi, w2_lo, h_parts = sb("w2_hi", [2 * F, HID], f32r), sb("w2_lo", [F, HID], f32r), sb("h_parts", [2 * F, CP], f32r)
        from_i = [sb(f"from_{i}", [128, NT, 2], i32) for i in range(2)]
        to_i = [sb(f"to_{i}", [128, NT, 2], i32) for i in range(2)]
        xg = [sb(f"xg_{i}", [128, NT, HID]) for i in range(2)]
        xgT = sb("xgT", [128, NC, CP])
        h3, g13, eg = (sb(nm, [F, CP]) for nm in ("h3", "g13", "eg"))
        yb = [sb(f"yb_{i}", [128, NT, HID]) for i in range(2)]
        T_B, H_B, Y_B = pb[0:3], pb[3:5], pb[5:8]

        s_tot, s_min, s_n = sem("totals_done"), sem("totals_clipped"), sem("first_n_done")
        d_join = [sem("d_joined_even"), sem("d_joined_odd")]
        d_join0 = [sem("d_joined_0"), sem("d_joined_1")]
        d_w13 = [sem(f"d_w13_{i}") for i in range(2)]
        d_w2 = [sem(f"d_w2_{i}") for i in range(2)]
        d_from = [sem(f"d_from{i}") for i in range(2)]
        d_to = [sem(f"d_to{i}") for i in range(2)]
        d_g = [[sem(f"d_gathered{i}_{t}") for t in range(NT)] for i in range(2)]
        d_add = [sem(f"d_added{i}") for i in range(2)]
        w2_hi_done, w2_lo_done, down_done = sem("w2_hi_done"), sem("w2_lo_done"), sem("down_done")
        xg_used = [sem(f"xg_used{i}") for i in range(2)]
        s_z = sem("xg_zeroed")
        tr_done, ev_done = sem("xg_transposed"), sem("xgT_copied")
        y_done = [sem("y_even"), sem("y_odd")]
        yev_done = [sem("yb_even"), sem("yb_odd")]
        h_done, h3_done, g_done, e_done, dn_done, rc_done, hs_done, hh_done, hl_done = (sem(nm) for nm in (
            "h_done", "h3_copied", "g13_done", "exp_g_done", "den_done", "recip_done", "h_silu_done", "h_hi", "h_lo"))
        block = ctx.enter_context(nc.Block())
        FULL = CAP // NT
        HALF = [(0, 512), (512, CP)]
        CNT = [(NT + 1) // 2, NT // 2]
        PAIRS = E // 2


        def join(eng, e):
            n = eng.value_load(first_n[0:1, e:e + 1], min_val=0, max_val=CAP)
            eng.dma_start(table_d[bass.ds(n + e * STRIDE, CP), :],
                          table_d[LIST1 + e * CP:LIST1 + (e + 1) * CP, :]).then_inc(
                              d_join0[e] if e < 2 else d_join[e % 2], 16)

        @block.sync
        def _(sp):
            def load_w13(j, i):
                sp.dma_start(w13_s[i][:, :, :], w13[2 * j + i]).then_inc(d_w13[i], 16)

            def load_w2(j, i):
                for half in (slice(0, F), slice(F, 2 * F)):
                    sp.dma_start(w2_s[i][half, :], w2T[2 * j + i]).then_inc(d_w2[i], 16)

            def entries(j, i):
                return table_d[bass.ds((2 * j + i) * STRIDE, CAP), :].rearrange("(p t) o -> p t o", t=NT)

            def load_from(j, i):
                sp.dma_start(from_i[i][0:FULL, :, :], entries(j, i)).then_inc(d_from[i], 16)

            def load_to(j, i):
                sp.dma_start(to_i[i][0:FULL, :, :], entries(j, i)).then_inc(d_to[i], 16)

            def ahead_3(j, i):
                n = (j + 1 + i, 1 - i)
                wait_apart(sp, (xg_used[1 - i], j + i + 1))
                load_from(*n)
                wait_apart(sp, (h_done, 2 * (2 * j + i + 2)))
                load_w13(*n)

            def ahead_2(j, i):
                wait_apart(sp, (w2_lo_done, 2 * j + i + 1))
                load_w2(j + 1, i)

            def ahead_1(j, i):
                wait_apart(sp, (d_add[1 - i], 16 * NT * (j + i)))
                load_to(j + i, 1 - i)

            for i in range(2):
                load_w13(0, i)
                load_w2(0, i)
            sp.wait_ge(s_n, 1)
            join(sp, 0)
            join(sp, 2)
            sp.wait_ge(s_z, 4)
            sp.wait_ge(d_join0[0], 16)
            load_from(0, 0)
            join(sp, 4)
            sp.wait_ge(d_join0[1], 16)
            load_from(0, 1)
            for e in range(6, E, 2):
                join(sp, e)
            for i in range(2):
                load_to(0, i)
            for p in range(2):
                sp.wait_ge(d_join[p], 16 * (E // 2 - 1))
            sp.wait_ge(xg_used[0], 1)
            load_from(1, 0)
            sp.wait_ge(h_done, 2)
            load_w13(1, 0)
            for i in range(2):
                ahead_3(0, i)
                ahead_2(0, i)
                if i == 1:
                    ahead_1(0, i)
            with sp.Fori(1, PAIRS - 2) as j:
                for i in range(2):
                    ahead_3(j, i)
                    ahead_2(j, i)
                    ahead_1(j, i)
            ahead_3(PAIRS - 2, 0)
            for i in range(2):
                ahead_2(PAIRS - 2, i)
                ahead_1(PAIRS - 2, i)
            ahead_1(PAIRS - 1, 0)

        @block.gpsimd
        def _(pool):
            def gather(j, i):
                wait_apart(pool, (d_from[i], 16 * j + 16), (xg_used[i], j))
                for t in range(NT):
                    nc.gpsimd.indirect_dma_start(
                        out=xg[i][:, t, :], out_offset=None, in_=xn2_d,
                        in_offset=bass.IndirectOffsetOnAxis(ap=from_i[i][:, t, 0:1], axis=0),
                        bounds_check=T - 1, oob_is_err=False).then_inc(d_g[i][t], 16)

            def scatter_add(j, i):
                e = 2 * j + i
                wait_apart(pool, (d_to[i], 16 * j + 16), (d_add[1 - i], 16 * NT * (j + i)))
                for t in range(NT):
                    wait_apart(pool, (yev_done[t % 2], CNT[t % 2] * e + t // 2 + 1))
                    nc.gpsimd.indirect_dma_start(
                        out=out, out_offset=bass.IndirectOffsetOnAxis(ap=to_i[i][:, t, 0:1], axis=0),
                        in_=yb[i][:, t, :], in_offset=None, compute_op=ALU.add).then_inc(d_add[i], 16)

            for tile in from_i + to_i:
                nc.gpsimd.memset(tile[:, :, 1], 0)
                nc.gpsimd.iota(tile[:, :, 0], pattern=[[1, NT]], base=T, channel_multiplier=NT).then_inc(s_z, 1)
            for i in range(2):
                nc.gpsimd.memset(xg[i][:, :, :], 0.0).then_inc(s_z, 1)
            pool.wait_ge(s_z, 6)
            for e in range(3):
                gather(e // 2, e % 2)
            for e in range(2):
                gather((e + 3) // 2, (e + 3) % 2)
                scatter_add(0, e)
            with pool.Fori(1, PAIRS - 2) as j:
                for i in range(2):
                    gather(j + 1 + i, 1 - i)
                    scatter_add(j, i)
            gather(PAIRS - 1, 1)
            for e in range(E - 4, E):
                scatter_add(e // 2, e % 2)
            for i in range(2):
                pool.wait_ge(d_add[i], 16 * NT * PAIRS)

        @block.tensor
        def _(pe):
            def transposes(j, i):
                e = 2 * j + i
                for t in range(NT):
                    pe.wait_ge(d_g[i][t], 16 * (j + 1))
                    wait(pe, ev_done, NT * e + max(0, t - 2))
                    for c in range(NC):
                        tr = nc.tensor.transpose(T_B[t % 3][:, c * 128:(c + 1) * 128],
                                                 xg[i][:, t, c * 128:(c + 1) * 128], ident[:, :])
                    tr.then_inc(tr_done, 1)

            def up(j, i):
                e = 2 * j + i
                pe.wait_ge(tr_done, NT * (e + 1))
                pe.sem_inc(xg_used[i], 1)
                pe.wait_ge(d_w13[i], 16 * (j + 1))
                for k, (lo, hi) in enumerate(HALF):
                    pe.wait_ge(ev_done, NT * e + hi // 128)
                    wait(pe, g_done, 2 * e)
                    for c in range(NC):
                        mm = nc.tensor.matmul(H_B[k][:, 0:hi - lo], w13_s[i][:, c, :], xgT[:, c, lo:hi],
                                              start=(c == 0), stop=(c == NC - 1))
                    mm.then_inc(h_done, 1)

            def down(j, i):
                e = 2 * j + i
                pe.wait_ge(w2_lo_done, e + 1)
                for t in range(NT):
                    p = t % 2
                    if t < 3:
                        for q in range(2):
                            wait(pe, yev_done[q], CNT[q] * e)
                    else:
                        pe.wait_ge(yev_done[1 - p], CNT[1 - p] * e + (t - 3) // 2 + 1)
                    cols = slice(t * 128, (t + 1) * 128)
                    pe.wait_ge(hl_done, 2 * e + (1 if cols.stop <= 512 else 2))
                    nc.tensor.matmul(Y_B[t % 3][:, :], h_parts[:, cols], w2_hi[:, :], start=True, stop=False)
                    nc.tensor.matmul(Y_B[t % 3][:, :], h_parts[0:F, cols], w2_lo[:, :],
                                     start=False, stop=True).then_inc(y_done[p], 1)
                pe.wait_ge(y_done[(NT - 1) % 2], CNT[(NT - 1) % 2] * (e + 1))
                pe.sem_inc(down_done, 1)

            def step(j, i, more=True):
                if more:
                    transposes(j + i, 1 - i)
                    up(j + i, 1 - i)
                down(j, i)

            nc.tensor.matmul(pb[0][:, 0:2 * E], ones_b[:, :], macc[:, :], start=True, stop=True).then_inc(s_tot, 1)
            transposes(0, 0)
            up(0, 0)
            step(0, 0)
            step(0, 1)
            with pe.Fori(1, PAIRS - 1) as j:
                step(j, 0)
                step(j, 1)
            step(PAIRS - 1, 0)
            step(PAIRS - 1, 1, more=False)

        def weigh_outputs(eng, scaled, p, j, i, between=None):
            e = 2 * j + i
            wait(eng, d_to[i], 16 * j + 16)
            wait(eng, d_add[i], 16 * NT * j)
            for n, t in enumerate(range(p, NT, 2)):
                eng.wait_ge(y_done[p], CNT[p] * e + n + 1)
                scaled(yb[i][:, t, :], Y_B[t % 3][:, :], to_i[i][:, t, 1:2].bitcast(f32)).then_inc(yev_done[p], 1)
                if between and n == 1:
                    between()

        @block.scalar
        def _(act):
            def split_h(e, k):
                lo, hi = HALF[k]
                act.wait_ge(hs_done, 2 * e + k + 1)
                wait(act, down_done, e)
                nc.scalar.copy(h_parts[0:F, lo:hi], g13[:, lo:hi]).then_inc(hh_done, 1)

            def first_half(j, i, more=True):
                e = 2 * j + i
                wait(act, h_done, 2 * e)
                for t in range(NT):
                    act.wait_ge(tr_done, NT * e + t + 1)
                    nc.scalar.copy(xgT[:, :, t * 128:(t + 1) * 128],
                                   T_B[t % 3][:, :].rearrange("p (c t) -> p c t", c=NC)).then_inc(ev_done, 1)
                wait(act, g_done, 2 * e)
                for k, (lo, hi) in enumerate(HALF):
                    if more:
                        split_h(e - 1, k)
                    act.wait_ge(h_done, 2 * e + k + 1)
                    nc.scalar.copy(h3[:, lo:hi], H_B[k][F:2 * F, 0:hi - lo]).then_inc(h3_done, 1)

            def split_w2(j, i):
                act.wait_ge(d_w2[i], 32 * (j + 1))
                wait(act, down_done, 2 * j + i)
                nc.scalar.copy(w2_hi[:, :], w2_s[i][:, :]).then_inc(w2_hi_done, 1)

            def exp_g(j, i):
                e = 2 * j + i
                act.wait_ge(g_done, 2 * e + 2)
                wait(act, hs_done, 2 * e)
                nc.scalar.activation(eg[:, :], g13[:, :], ACT.Exp, scale=-1.0).then_inc(e_done, 1)

            def step(j, i, more=True):
                if more:
                    first_half(j + i, 1 - i)
                else:
                    for k in range(2):
                        split_h(2 * j + i, k)
                weigh_outputs(act, lambda o, x, w: nc.scalar.activation(o, x, ACT.Copy, scale=w), 0, j, i,
                              between=(lambda: exp_g(j + i, 1 - i)) if more else None)
                if more:
                    split_w2(j + i, 1 - i)

            act.wait_ge(s_n, 1)
            for e in range(1, E, 2):
                join(act, e)
            first_half(0, 0, more=False)
            exp_g(0, 0)
            split_w2(0, 0)
            step(0, 0)
            step(0, 1)
            with act.Fori(1, PAIRS - 1) as j:
                step(j, 0)
                step(j, 1)
            step(PAIRS - 1, 0)
            step(PAIRS - 1, 1, more=False)

        @block.vector
        def _(dve):
            def products(j, i):
                e = 2 * j + i
                wait(dve, hl_done, 2 * e)
                for k, (lo, hi) in enumerate(HALF):
                    dve.wait_ge(h3_done, 2 * e + k + 1)
                    nc.vector.tensor_tensor(g13[:, lo:hi], H_B[k][0:F, 0:hi - lo], h3[:, lo:hi],
                                            ALU.mult).then_inc(g_done, 1)

            def silu(j, i):
                e = 2 * j + i
                dve.wait_ge(e_done, e + 1)
                nc.vector.tensor_scalar(eg[:, :], eg[:, :], 1.0, None, ALU.add).then_inc(dn_done, 1)
                dve.wait_ge(dn_done, e + 1)
                for k, (lo, hi) in enumerate(HALF):
                    nc.vector.reciprocal(eg[:, lo:hi], eg[:, lo:hi]).then_inc(rc_done, 1)
                    dve.wait_ge(rc_done, 2 * e + k + 1)
                    nc.vector.tensor_tensor(g13[:, lo:hi], g13[:, lo:hi], eg[:, lo:hi], ALU.mult).then_inc(hs_done, 1)
                    if k == 0:
                        dve.wait_ge(w2_hi_done, e + 1)
                        nc.vector.tensor_tensor(w2_lo[:, :], w2_s[i][0:F, :], w2_hi[0:F, :].bitcast(f32),
                                                ALU.subtract).then_inc(w2_lo_done, 1)
                for k, (lo, hi) in enumerate(HALF):
                    dve.wait_ge(hh_done, 2 * e + k + 1)
                    nc.vector.tensor_tensor(h_parts[F:2 * F, lo:hi], g13[:, lo:hi], h_parts[0:F, lo:hi].bitcast(f32),
                                            ALU.subtract).then_inc(hl_done, 1)

            def step(j, i, more=True):
                if more:
                    products(j + i, 1 - i)
                weigh_outputs(dve, lambda o, x, w: nc.vector.tensor_scalar(o, x, w, None, ALU.mult), 1, j, i)
                if more:
                    silu(j + i, 1 - i)

            dve.wait_ge(s_tot, 1)
            nc.vector.tensor_scalar(tot[:, :], pb[0][:, 0:E], float(CAP), None, ALU.min).then_inc(s_min, 1)
            dve.wait_ge(s_min, 1)
            nc.vector.tensor_copy(first_n[:, :], tot[:, :]).then_inc(s_n, 1)
            products(0, 0)
            silu(0, 0)
            step(0, 0)
            step(0, 1)
            with dve.Fori(1, PAIRS - 1) as j:
                step(j, 0)
                step(j, 1)
            step(PAIRS - 1, 0)
            step(PAIRS - 1, 1, more=False)


def build(nc, x, xT, cT, wq, wk, wv, wo, qw, kw, gateT, w13, w2T, out):
    f32, f32r, bf16, i32, u32 = (mybir.dt.float32, mybir.dt.float32r, mybir.dt.bfloat16,
                                 mybir.dt.int32, mybir.dt.uint32)
    ACT = mybir.ActivationFunctionType
    AX = mybir.AxisListType

    xn2_d = nc.dram_tensor("xn2_scratch", (T, HID), f32, kind="Internal").ap()
    table_d = nc.dram_tensor("token_table", (ROWS, 2), i32, kind="Internal").ap()

    def wait(eng, sem, n, apart=False):
        if isinstance(n, int) and n <= 0:
            return
        if apart:
            wait_apart(eng, (sem, n))
        else:
            eng.wait_ge(sem, n)

    def wait_apart(eng, *pairs):
        with ExitStack() as regs:
            values = []
            for s, n in pairs:
                if not isinstance(n, int):
                    reg = regs.enter_context(eng.register(f"wait_{s.name}_{nc.next_id()}"))
                    eng.reg_add(reg, n, 0)
                    n = reg
                values.append((s, n))
            eng.wait_ge(s_const, 1)
            for s, n in values:
                if not (isinstance(n, int) and n <= 0):
                    eng.wait_ge(s, n)

    keep = ExitStack()
    with keep:
        def sem(name):
            return keep.enter_context(nc.semaphore(name))

        def psum(name):
            return keep.enter_context(nc.psum_tensor(name, [128, 512], f32))

        ident = keep.enter_context(nc.sbuf_tensor("ident", [128, 128], f32))
        ones_b = keep.enter_context(nc.sbuf_tensor("ones_b", [128, 128], bf16))
        macc = keep.enter_context(nc.sbuf_tensor("macc", [128, 2 * E], bf16))
        pb = [psum(f"pb{i}") for i in range(8)]
        s_table, s_const = sem("s_table_scattered"), sem("s_const")

        with ExitStack() as ctx:
            def sb(name, shape, dt=f32):
                return ctx.enter_context(nc.sbuf_tensor(name, shape, dt))

            wqp = [sb(f"wq_{p}", [128, NC, NH * HD], f32r) for p in ("hi", "lo")]
            wkvp = [sb(f"wkv_{p}", [128, 2, NC, NG * HD], f32r) for p in ("hi", "lo")]
            wop = [sb(f"wo_{p}", [128, NH, HID], f32r) for p in ("hi", "lo")]
            xp = [sb(f"x_{p}", [128, NC, 128], f32r) for p in ("hi", "lo")]
            cp = [sb(f"c_{p}", [128, NC, 128], f32r) for p in ("hi", "lo")]
            qp = [sb(f"q_{p}", [128, HPG, 128], f32r) for p in ("hi", "lo")]
            k_parts = sb("k_parts", [128, NG, 2, 128], f32r)
            kp = [k_parts[:, :, p, :] for p in range(2)]
            vp = [sb(f"v_{p}", [128, NG, HD], f32r) for p in ("hi", "lo")]
            ptp = [sb(f"pt_{p}", [128, HPG, 128], f32r) for p in ("hi", "lo")]
            otp = [sb(f"ot_{p}", [128, HPG, 128], f32r) for p in ("hi", "lo")]
            work = sb("work", [128, 8, 512])
            q_nat, probs, k_nat, xn2 = (work[:, i, :] for i in range(4))
            raw, x_stat, x_res = (work[:, i, :] for i in range(4, 7))
            junk = work[:, 7, :].rearrange("p (h t) -> p h t", h=4)
            xn2T = k_nat
            tri = sb("tri", [128, 128], bf16)
            gate = sb("gate", [128, NC, E])
            iota12 = sb("iota12", [128, E])
            mean_w = sb("mean_w", [128, 128])
            sentinel = sb("sentinel", [128, NT, 2], i32)

            small = sb("small", [128, 160])
            at = [0]

            def sm(n, dt=f32):
                v = small[:, at[0]:at[0] + n]
                at[0] += n
                return v if dt is f32 else v.bitcast(dt)

            smax, nmax, psums, rsums = sm(4), sm(4), sm(4), sm(4)
            q_ssq, q_ms, q_rms = sm(4), sm(4), sm(4)
            k_ssq, k_ms, k_rms = sm(4), sm(4), sm(4)
            neghalf = sm(4)
            bn_x, mv_x, eps_x = sm(6), sm(2), sm(1)
            bn_2, mv_2, ve_2, rstd_2 = sm(6), sm(2), sm(1), sm(1)
            wqk, qw_s, kw_s = sm(1), sm(1), sm(1)
            lg, top8, idx8, idxf = sm(E), sm(8), sm(8, u32), sm(2)
            mask = sm(E, bf16)
            posm, pos2, over = sm(2 * E), sm(2), sm(2)
            dst, tokf, entry = sm(2, i32), sm(1), sm(4, i32)
            entry_t = entry.rearrange("p (k o) -> p k o", k=2)
            diff, e10, den = sm(1), sm(1), sm(1)
            list_off = sm(2)

            Q_B, V_B, S0_B, S1_B, PT_B, QT_B, OT_B, WO_B = pb

            d_w = [sem(f"d_w_stage{i}") for i in range(5)]
            d_small, d_c, d_x, d_xs, d_xr = sem("d_small"), sem("d_c"), sem("d_x"), sem("d_xs"), sem("d_xr")
            d_x1, d_xn2, d_sent = sem("d_x1_stored"), sem("d_xn2_stored"), sem("d_sentinel")
            s_mw, s_zero = sem("s_mw"), sem("s_zero")
            df_done, e10_done, den_done, w0_done, w1_done = (sem(n) for n in (
                "diff_done", "exp_diff_done", "den10_done", "w0_done", "w1_done"))
            w_mean, w_cent, w_hi, w_lo = sem("w_mean"), sem("w_centred"), sem("w_hi"), sem("w_lo")
            wqk_done = sem("wqk_done")
            c_hi, c_lo, x_hi, x_lo = sem("c_hi"), sem("c_lo"), sem("x_hi"), sem("x_lo")
            k_done, v_done, q_done = sem("k_done"), sem("v_done"), sem("q_done")
            k_cp, k_sq, k_m, k_r, k_sc, k_tr, k_hi, k_lo = (sem(n) for n in (
                "k_copied", "k_squared", "k_meansq", "k_rms", "k_scaled", "k_transposed", "k_hi", "k_lo"))
            v_hi, v_lo = sem("v_hi"), sem("v_lo")
            q_cp, q_sq, q_m, q_r, q_tr, q_hi, q_lo = (sem(n) for n in (
                "q_copied", "q_squared", "q_meansq", "q_rms", "q_transposed", "q_hi", "q_lo"))
            sc_half, s2_cp = sem("scores_half"), sem("scores_copied")
            sc_done, mx_done, nm_done, exp_done, rs_done, p_done = (sem(n) for n in (
                "scores_done", "max_done", "negmax_done", "exp_done", "rsum_done", "probs_done"))
            pt_done, pt_hi, pt_lo, ot_done, ot_hi, ot_lo = (sem(n) for n in (
                "pt_done", "pt_hi", "pt_lo", "ot_done", "ot_hi", "ot_lo"))
            wo_used, x1_done, b2_done, mv2_done, ve2_done, r2_done, xn2_done = (sem(n) for n in (
                "wo_used", "x1_done", "bn2_done", "mv2_done", "ve2_done", "rstd2_done", "xn2_done"))
            bx_done, mvx_done, eps_done = sem("bnx_done"), sem("mvx_done"), sem("eps_done")
            xt_done, xt_cp, lg_done, lg_cp, t8, i8, ixf, mk = (sem(n) for n in (
                "xn2T_done", "xn2T_copied", "logits_done", "logits_copied", "top8_done", "idx8_done",
                "idxf_done", "mask_done"))
            pos_done, pm, p2, ov, ovb, d0, dst_rdy, tok_i, tok_n, mac = (sem(n) for n in (
                "pos_done", "pos_masked", "pos_reduced", "over_done", "over_big", "dst_summed",
                "dst_ready", "token_ids", "token_next", "macc_done"))

            block = ctx.enter_context(nc.Block())

            LOTS = ([("k", n) for n in range(NG)] + [("v", n) for n in range(NG)] + [("q", n) for n in range(NH)]
                    + [("o", n) for n in range(NH)])
            NLOT = len(LOTS)
            V_IN, Q_IN = 2 * NG, 2 * NG
            STAGES = (0, 1, 3, 6, 7)
            NST = len(STAGES)

            def stage(l):
                flat = work[:, STAGES[l % NST], :]
                return flat if LOTS[l][0] == "o" else flat.rearrange("p (c n) -> p c n", c=NC)

            def lot_parts(l):
                kind, n = LOTS[l]
                cols = slice(n * 128, (n + 1) * 128)
                if kind in "kv":
                    return [w[:, "kv".index(kind), :, cols] for w in wkvp]
                if kind == "q":
                    return [w[:, :, cols] for w in wqp]
                return [w[:, n, :] for w in wop]

            def lot_landed(eng, l):
                eng.wait_ge(d_w[l % NST], 16 * (l // NST + 1))

            def mean_cols(n):
                return (S0_B, S1_B, PT_B, QT_B)[n % 4][:, 0:128]

            @block.sync
            def _(sp):
                raw_v = raw.rearrange("p (c t) -> p c t", c=NC)

                def load_c(b):
                    wait(sp, x_lo, b)
                    sp.dma_start(raw_v, cT[b]).then_inc(d_c, 16)

                def load_x(b):
                    wait(sp, c_lo, b + 1)
                    sp.dma_start(raw_v, xT[b]).then_inc(d_x, 16)

                def load_stat(b):
                    wait(sp, bx_done, b)
                    sp.dma_start(x_stat, x[b]).then_inc(d_xs, 16)

                def load_res(b):
                    wait_apart(sp, (xn2_done, b), (d_x1, 16 * b))
                    sp.dma_start(x_res, x[b]).then_inc(d_xr, 16)

                def store_x1(b):
                    wait(sp, x1_done, b + 1)
                    sp.dma_start(out[bass.ds(b * 128, 128), :], x_res).then_inc(d_x1, 16)

                def store_xn2(b):
                    wait_apart(sp, (xn2_done, b + 1))
                    sp.dma_start(xn2_d[bass.ds(b * 128, 128), :], xn2).then_inc(d_xn2, 16)

                wkv_v = [w.rearrange("(c p) n -> p c n", p=128) for w in (wk, wv)]
                wq_v = wq.rearrange("(c p) n -> p c n", p=128)
                for l, (kind, n) in enumerate(LOTS):
                    if l == NG:
                        load_c(0)
                        load_stat(0)
                    if l == V_IN:
                        sp.dma_start(gate[:, :, :], gateT).then_inc(d_small, 16)
                        sp.dma_start(qw_s, qw).then_inc(d_small, 16)
                        sp.dma_start(kw_s, kw).then_inc(d_small, 16)
                    if l == Q_IN + NG:
                        load_x(0)
                    if l >= NST:
                        sp.wait_ge(w_lo, l - NST + 1)
                    cols = slice(n * 128, (n + 1) * 128)
                    src = (wo[cols, :] if kind == "o" else wq_v[:, :, cols] if kind == "q"
                           else wkv_v["kv".index(kind)][:, :, cols])
                    sp.dma_start(stage(l), src).then_inc(d_w[l % NST], 16)
                sp.wait_ge(s_const, 1)
                sp.dma_start(table_d[LIST1:, :].rearrange("(e p t) o -> p e (t o)", p=128, t=NT),
                             sentinel[:, :, :].rearrange("p t o -> p (t o)")[:, None, :].broadcast_to(
                                 [128, E, 2 * NT])).then_inc(d_sent, 16)
                sp.dma_start(out[T:T + CP, :], x.rearrange("b t n -> (b t) n")[0:CP, :]).then_inc(d_sent, 16)
                sp.wait_ge(w_lo, NLOT)
                load_res(0)

                def body(b, first=False, last=False):
                    if not last:
                        load_c(b + 1)
                        load_stat(b + 1)
                    if not first:
                        store_x1(b - 1)
                    if not last:
                        load_x(b + 1)
                    if not first:
                        store_xn2(b - 1)
                        load_res(b)

                body(0, first=True)
                body(1)
                with sp.Fori(2, NB - 1) as b:
                    body(b)
                body(NB - 1, last=True)
                store_x1(NB - 1)
                store_xn2(NB - 1)
                sp.wait_ge(d_x1, 16 * NB)
                sp.wait_ge(d_xn2, 16 * NB)
                sp.wait_ge(d_sent, 32)

            @block.tensor
            def _(pe):
                pe.wait_ge(s_mw, 1)
                def mean(n):
                    l = Q_IN + n
                    lot_landed(pe, l)
                    wait(pe, w_cent, n - 3)
                    for c in range(NC):
                        mm = nc.tensor.matmul(mean_cols(n), mean_w[:, :], stage(l)[:, c, :],
                                              start=(c == 0), stop=(c == NC - 1))
                    mm.then_inc(w_mean, 1)

                PARTS = ((0, 0), (0, 1), (1, 0))

                def project(bank, lhs, rhs):
                    n = 0
                    for c in range(NC):
                        for a, b_ in PARTS:
                            mm = nc.tensor.matmul(bank[:, :], lhs[a][:, c, :], rhs[b_][:, c, :],
                                                  start=(n == 0), stop=(n == 3 * NC - 1))
                            n += 1
                    return mm

                def weights_in(b, n):
                    if isinstance(b, int) and b == 0:
                        pe.wait_ge(w_lo, n)

                def keys(b):
                    weights_in(b, NG)
                    wait(pe, c_lo, b + 1)
                    wait(pe, q_cp, 4 * b)
                    project(Q_B, cp, [w[:, 0, :, :] for w in wkvp]).then_inc(k_done, 1)

                def values(b):
                    weights_in(b, V_IN)
                    wait(pe, lg_cp, b - 1)
                    wait(pe, v_lo, b)
                    project(V_B, cp, [w[:, 1, :, :] for w in wkvp]).then_inc(v_done, 1)

                def queries(b, g):
                    weights_in(b, Q_IN + HPG * (g + 1))
                    if g == 0:
                        wait(pe, x_lo, b + 1)
                    wait(pe, q_cp, 4 * b + g)
                    if g == 0:
                        wait(pe, k_cp, b + 1)
                    if g == 1:
                        wait(pe, k_lo, b + 1)
                    project(Q_B, xp, [w[:, :, g * 512:(g + 1) * 512] for w in wqp]).then_inc(q_done, 1)

                def transpose_q(b, g):
                    u = 4 * b + g
                    wait(pe, q_cp, u + 1)
                    wait(pe, q_lo, u)
                    for h in range(HPG):
                        tr = nc.tensor.transpose(QT_B[:, h * 128:(h + 1) * 128],
                                                 q_nat[:, h * 128:(h + 1) * 128], ident[:, :])
                    tr.then_inc(q_tr, 1)

                def transpose_k(b):
                    wait(pe, k_sc, b + 1)
                    wait(pe, q_cp, 4 * b + 1)
                    for g in range(NG):
                        tr = nc.tensor.transpose(Q_B[:, g * 128:(g + 1) * 128],
                                                 k_nat[:, g * 128:(g + 1) * 128], ident[:, :])
                    tr.then_inc(k_tr, 1)

                def scores(b, g):
                    u = 4 * b + g
                    if g == 0:
                        wait(pe, k_lo, b + 1)
                    wait(pe, q_lo, u + 1)
                    wait(pe, mx_done, u)
                    for h in range(HPG):
                        bank, at_h = (S0_B, S1_B)[h // 2], 256 * (h % 2)
                        nc.tensor.matmul(bank[:, at_h:at_h + 256], qp[0][:, h, :], k_parts[:, g, :, :],
                                         start=True, stop=False)
                        mm = nc.tensor.matmul(bank[:, at_h:at_h + 128], qp[1][:, h, :], kp[0][:, g, :],
                                              start=False, stop=True)
                        if h == 1:
                            mm.then_inc(sc_half, 1)
                    mm.then_inc(sc_done, 1)

                def transpose_p(b, g):
                    u = 4 * b + g
                    wait(pe, p_done, u + 1)
                    wait(pe, pt_lo, u)
                    for h in range(HPG):
                        tr = nc.tensor.transpose(PT_B[:, h * 128:(h + 1) * 128],
                                                 probs[:, h * 128:(h + 1) * 128], ident[:, :])
                    tr.then_inc(pt_done, 1)

                def attend(b, g):
                    u = 4 * b + g
                    wait(pe, v_lo, b + 1)
                    wait(pe, pt_lo, u + 1)
                    wait(pe, ot_lo, u)
                    if g == 3:
                        wait(pe, pos_read_count, b)
                    for n, (a, b_) in enumerate(PARTS):
                        mm = nc.tensor.matmul(OT_B[:, :], vp[a][:, g, :], ptp[b_][:, :, :],
                                              start=(n == 0), stop=(n == 2))
                    mm.then_inc(ot_done, 1)

                def out_project(b, g, h):
                    u = 4 * b + g
                    weights_in(b, Q_IN + NH + HPG * g + h + 1)
                    if h == 0:
                        wait(pe, ot_lo, u + 1)
                        if g == 0:
                            wait(pe, x1_done, b)
                    for n, (a, b_) in enumerate(PARTS):
                        mm = nc.tensor.matmul(WO_B[:, :], otp[a][:, h, :], wop[b_][:, g * HPG + h, :],
                                              start=(g == 0 and h == 0 and n == 0),
                                              stop=(g == NG - 1 and h == HPG - 1 and n == 2))
                    if h == HPG - 1:
                        mm.then_inc(wo_used, 1)

                def transpose_x(b, last=False):
                    wait(pe, xn2_done, b + 1)
                    if not last:
                        wait(pe, v_lo, b + 2)
                    for c in range(NC):
                        tr = nc.tensor.transpose(V_B[:, c * 128:(c + 1) * 128],
                                                 xn2[:, c * 128:(c + 1) * 128], ident[:, :])
                    tr.then_inc(xt_done, 1)

                def route(b):
                    wait(pe, xt_cp, b + 1)
                    for c in range(NC):
                        mm = nc.tensor.matmul(V_B[:, 0:E], xn2T[:, c * 128:(c + 1) * 128], gate[:, c, :],
                                              start=(c == 0), stop=(c == NC - 1))
                    mm.then_inc(lg_done, 1)

                def positions(b, last=False):
                    wait(pe, mk, b + 1)
                    wait(pe, mac, b + 1)
                    wait(pe, ot_lo, NU if last else 4 * b + 7)
                    nc.tensor.matmul(OT_B[:, 0:2 * E], tri[:, :], mask, start=True, stop=False)
                    nc.tensor.matmul(OT_B[:, 0:2 * E], ones_b[:, :], macc[:, :],
                                     start=False, stop=True).then_inc(pos_done, 1)

                pos_read_count = pm
                for n in range(NH):
                    mean(n)
                    if n == 3:
                        keys(0)
                    if n == 7:
                        values(0)
                    if n == NH - 1:
                        queries(0, 0)
                pe.wait_ge(s_const, 1)
                pe.wait_ge(d_small, 48)
                transpose_k(0)
                transpose_q(0, 0)

                def body(b, first=False, last=False):
                    for g in range(NG):
                        has_prev = not (first and g == 0)
                        has_next = not (last and g == NG - 1)
                        prev = (b, g - 1) if g else (b - 1, NG - 1)
                        nxt = (b, g + 1) if g < NG - 1 else (b + 1, 0)
                        scores(b, g)
                        if has_prev:
                            attend(*prev)
                        if g == 3 and not last:
                            keys(b + 1)
                            values(b + 1)
                        if has_next:
                            queries(*nxt)
                        if g == 2 and not first:
                            transpose_x(b - 1)
                        if has_prev:
                            out_project(*prev, 0)
                        if has_prev:
                            out_project(*prev, 1)
                        if g == 3 and not last:
                            transpose_k(b + 1)
                        if has_next:
                            transpose_q(*nxt)
                        transpose_p(b, g)
                        if g == 2 and not first:
                            route(b - 1)
                        if g == 3 and not first:
                            positions(b - 1)
                        if has_prev:
                            out_project(*prev, 2)
                            out_project(*prev, 3)

                body(0, first=True)
                body(1)
                with pe.Fori(2, NB - 1) as b:
                    body(b)
                body(NB - 1, last=True)
                attend(NB - 1, NG - 1)
                for h in range(HPG):
                    out_project(NB - 1, NG - 1, h)
                transpose_x(NB - 1, last=True)
                route(NB - 1)
                positions(NB - 1, last=True)

            @block.scalar
            def _(act):
                raw_v = raw.rearrange("p (c t) -> p c t", c=NC)

                def split_c(b):
                    wait(act, d_c, 16 * (b + 1))
                    wait(act, v_done, b)
                    nc.scalar.copy(cp[0][:, :, :], raw_v).then_inc(c_hi, 1)

                def split_x(b):
                    wait(act, d_x, 16 * (b + 1))
                    wait(act, q_done, 4 * b)
                    nc.scalar.copy(xp[0][:, :, :], raw_v).then_inc(x_hi, 1)

                def copy_k(b):
                    wait(act, k_done, b + 1)
                    wait(act, k_tr, b)
                    wait(act, lg_done, b - 1)
                    nc.scalar.copy(k_nat, Q_B[:, :]).then_inc(k_cp, 1)

                def split_k(b):
                    wait(act, k_tr, b + 1)
                    wait(act, sc_done, 4 * b)
                    if isinstance(b, int) and b == 0:
                        act.wait_ge(wqk_done, 1)
                    nc.scalar.activation(kp[0], Q_B[:, :].rearrange("p (g t) -> p g t", g=NG),
                                         ACT.Copy, scale=wqk).then_inc(k_hi, 1)

                def split_v(b):
                    wait(act, v_done, b + 1)
                    wait(act, ot_done, 4 * b)
                    nc.scalar.copy(vp[0][:, :, :], V_B[:, :].rearrange("p (g t) -> p g t", g=NG)).then_inc(v_hi, 1)

                def copy_q(b, g):
                    u = 4 * b + g
                    wait(act, q_done, u + 1)
                    wait(act, q_tr, u)
                    wait(act, q_sq, u)
                    nc.scalar.copy(q_nat, Q_B[:, :]).then_inc(q_cp, 1)

                def split_q(b, g):
                    u = 4 * b + g
                    wait(act, q_tr, u + 1)
                    wait(act, sc_done, u)
                    nc.scalar.copy(qp[0][:, :, :], QT_B[:, :].rearrange("p (h t) -> p h t", h=HPG)).then_inc(q_hi, 1)

                def copy_s2(b, g):
                    u = 4 * b + g
                    wait(act, pt_done, u)
                    for k, done in enumerate((sc_half, sc_done)):
                        wait(act, done, u + 1)
                        nc.scalar.copy(probs[:, 256 * k:256 * k + 256].rearrange("p (h t) -> p h t", h=2),
                                       (S0_B, S1_B)[k][:, :].rearrange("p (h s t) -> p h s t", h=2, s=2)[:, :, 1, :]
                                       ).then_inc(s2_cp, 1)

                def exps(b, g):
                    u = 4 * b + g
                    wait(act, nm_done, u + 1)
                    for h in range(HPG):
                        ex = nc.scalar.activation(probs[:, h * 128:(h + 1) * 128], probs[:, h * 128:(h + 1) * 128],
                                                  ACT.Exp, bias=nmax[:, h:h + 1], scale=q_rms[:, h:h + 1],
                                                  accum_out=psums[:, h:h + 1])
                    ex.then_inc(exp_done, 1)

                def split_p(b, g):
                    u = 4 * b + g
                    wait(act, pt_done, u + 1)
                    wait(act, ot_done, u)
                    nc.scalar.copy(ptp[0][:, :, :], PT_B[:, :].rearrange("p (h t) -> p h t", h=HPG)).then_inc(pt_hi, 1)

                def split_o(b, g):
                    u = 4 * b + g
                    wait(act, ot_done, u + 1)
                    wait(act, wo_used, u)
                    nc.scalar.copy(otp[0][:, :, :], OT_B[:, :].rearrange("p (h t) -> p h t", h=HPG)).then_inc(ot_hi, 1)

                def exp_diff(b):
                    wait(act, df_done, b + 1)
                    wait(act, w1_done, b)
                    nc.scalar.activation(e10, diff, ACT.Exp).then_inc(e10_done, 1)

                def copy_xt(b, keys_after=True):
                    wait(act, xt_done, b + 1)
                    if keys_after:
                        wait(act, k_tr, b + 2)
                    nc.scalar.copy(xn2T, V_B[:, :]).then_inc(xt_cp, 1)

                for l, (kind, n) in enumerate(LOTS):
                    if kind == "q":
                        act.wait_ge(w_cent, n + 1)
                    else:
                        lot_landed(act, l)
                    nc.scalar.copy(lot_parts(l)[0], stage(l)).then_inc(w_hi, 1)
                    if l == V_IN - 1:
                        split_c(0)
                    if l == Q_IN + 2 * NG - 1:
                        split_x(0)
                        copy_k(0)
                act.wait_ge(w_lo, NLOT)
                copy_q(0, 0)
                split_k(0)
                split_q(0, 0)

                def body(b, first=False, last=False):
                    for g in range(NG):
                        prev = (b, g - 1) if g else (b - 1, NG - 1)
                        nxt = (b, g + 1) if g < NG - 1 else (b + 1, 0)
                        copy_s2(b, g)
                        if not (first and g == 0):
                            split_o(*prev)
                        exps(b, g)
                        if g == 3 and not last:
                            split_x(b + 1)
                            copy_k(b + 1)
                        if not (last and g == NG - 1):
                            copy_q(*nxt)
                        if g == 0:
                            split_v(b)
                        if g == 2 and not first:
                            copy_xt(b - 1)
                        if g == 3 and not first:
                            exp_diff(b - 1)
                        if g == 3 and not last:
                            split_k(b + 1)
                        if not (last and g == NG - 1):
                            split_q(*nxt)
                        split_p(b, g)
                        if g == 0 and not last:
                            split_c(b + 1)

                body(0, first=True)
                body(1)
                with act.Fori(2, NB - 1) as b:
                    body(b)
                body(NB - 1, last=True)
                split_o(NB - 1, NG - 1)
                copy_xt(NB - 1, keys_after=False)
                exp_diff(NB - 1)

            @block.vector
            def _(dve):
                def minus(part, whole):
                    return nc.vector.tensor_tensor(part[1], whole, part[0].bitcast(f32), ALU.subtract)

                nc.vector.memset(mean_w[:, :], 1.0 / HID).then_inc(s_mw, 1)
                nc.vector.memset(neghalf, -0.5)
                nc.vector.memset(macc[:, :], 0.0)
                nc.vector.memset(list_off[:, 0:1], 0.0)
                nc.vector.memset(list_off[:, 1:2], float(LIST1)).then_inc(mac, 1)
                raw_v = raw.rearrange("p (c t) -> p c t", c=NC)

                def view(bank, n=4):
                    return bank[:, :].rearrange("p (h t) -> p h t", h=n)

                def all3(parts):
                    return [p[:, :, :] for p in parts]

                def split_c(b):
                    wait(dve, c_hi, b + 1)
                    minus(all3(cp), raw_v).then_inc(c_lo, 1)

                def split_x(b):
                    wait(dve, x_hi, b + 1)
                    minus(all3(xp), raw_v).then_inc(x_lo, 1)

                def stats_x(b):
                    wait(dve, d_xs, 16 * (b + 1))
                    wait(dve, mvx_done, b)
                    nc.vector.bn_stats(bn_x, x_stat).then_inc(bx_done, 1)
                    wait(dve, bx_done, b + 1, apart=True)
                    wait(dve, eps_done, b)
                    nc.vector.bn_aggr(mv_x, bn_x).then_inc(mvx_done, 1)

                def square_k(b):
                    wait(dve, k_cp, b + 1)
                    wait(dve, k_m, b)
                    wait(dve, q_sq, 4 * b)
                    for g in range(NG):
                        kk = k_nat[:, g * 128:(g + 1) * 128]
                        sq = nc.vector.tensor_tensor_reduce(out=junk[:, g, :], in0=kk, in1=kk, scale=1.0, scalar=0.0,
                                                            op0=ALU.mult, op1=ALU.add, accum_out=k_ssq[:, g:g + 1])
                    sq.then_inc(k_sq, 1)

                def scale_k(b):
                    wait(dve, k_r, b + 1)
                    kv = k_nat.rearrange("p (g t) -> p g t", g=NG)
                    nc.vector.tensor_tensor(kv, kv, k_rms[:, :, None].broadcast_to([128, NG, 128]),
                                            ALU.mult).then_inc(k_sc, 1)

                def split_k(b):
                    wait(dve, k_hi, b + 1)
                    nc.vector.scalar_tensor_tensor(out=kp[1], in0=view(Q_B), scalar=wqk,
                                                   in1=kp[0].bitcast(f32), op0=ALU.mult,
                                                   op1=ALU.subtract).then_inc(k_lo, 1)

                def split_v(b):
                    wait(dve, v_hi, b + 1)
                    minus(all3(vp), view(V_B)).then_inc(v_lo, 1)

                def square_q(b, g):
                    u = 4 * b + g
                    wait(dve, q_cp, u + 1)
                    wait(dve, q_m, u)
                    if g == 0:
                        wait(dve, k_sq, b + 1)
                    for h in range(HPG):
                        qq = q_nat[:, h * 128:(h + 1) * 128]
                        sq = nc.vector.tensor_tensor_reduce(out=junk[:, h, :], in0=qq, in1=qq, scale=1.0, scalar=0.0,
                                                            op0=ALU.mult, op1=ALU.add, accum_out=q_ssq[:, h:h + 1])
                    sq.then_inc(q_sq, 1)

                def split_q(b, g):
                    wait(dve, q_hi, 4 * b + g + 1)
                    minus(all3(qp), view(QT_B)).then_inc(q_lo, 1)

                def maxima(b, g):
                    u = 4 * b + g
                    wait(dve, nm_done, u)
                    for h in range(HPG):
                        bank, at_h = (S0_B, S1_B)[h // 2], 256 * (h % 2)
                        if h % 2 == 0:
                            wait(dve, s2_cp, 2 * u + 1 + h // 2, apart=True)
                        mx = nc.vector.tensor_tensor_reduce(
                            out=probs[:, h * 128:(h + 1) * 128], in0=bank[:, at_h:at_h + 128],
                            in1=probs[:, h * 128:(h + 1) * 128], scale=1.0, scalar=LOWEST, op0=ALU.add, op1=ALU.max,
                            accum_out=smax[:, h:h + 1])
                    mx.then_inc(mx_done, 1)
                    wait(dve, mx_done, u + 1)
                    wait(dve, q_r, u + 1)
                    wait(dve, exp_done, u)
                    nc.vector.scalar_tensor_tensor(out=nmax, in0=smax, scalar=-1.0, in1=q_rms,
                                                   op0=ALU.mult, op1=ALU.mult).then_inc(nm_done, 1)

                def normalise(b, g):
                    u = 4 * b + g
                    wait(dve, exp_done, u + 1)
                    wait(dve, p_done, u)
                    nc.vector.reciprocal(rsums, psums).then_inc(rs_done, 1)
                    wait(dve, rs_done, u + 1)
                    pv = probs.rearrange("p (h t) -> p h t", h=HPG)
                    nc.vector.tensor_tensor(pv, pv, rsums[:, :, None].broadcast_to([128, HPG, 128]),
                                            ALU.mult).then_inc(p_done, 1)

                def split_p(b, g):
                    wait(dve, pt_hi, 4 * b + g + 1)
                    minus(all3(ptp), view(PT_B)).then_inc(pt_lo, 1)

                def split_o(b, g):
                    wait(dve, ot_hi, 4 * b + g + 1)
                    minus(all3(otp), view(OT_B)).then_inc(ot_lo, 1)

                def residual(b):
                    wait(dve, wo_used, 4 * b + 4)
                    wait(dve, d_xr, 16 * (b + 1))
                    nc.vector.tensor_tensor(x_res, x_res, WO_B[:, :], ALU.add).then_inc(x1_done, 1)

                def stats_2(b):
                    wait(dve, x1_done, b + 1)
                    nc.vector.bn_stats(bn_2, x_res).then_inc(b2_done, 1)
                    wait(dve, b2_done, b + 1, apart=True)
                    wait(dve, ve2_done, b)
                    wait(dve, xn2_done, b)
                    nc.vector.bn_aggr(mv_2, bn_2).then_inc(mv2_done, 1)

                def norm2(b):
                    wait(dve, r2_done, b + 1)
                    wait(dve, d_xn2, 16 * b)
                    wait(dve, xt_done, b)
                    nc.vector.tensor_scalar(xn2, x_res, mv_2[:, 0:1], rstd_2, ALU.subtract,
                                            ALU.mult).then_inc(xn2_done, 1)

                def copy_logits(b):
                    wait(dve, lg_done, b + 1)
                    nc.vector.tensor_copy(lg, V_B[:, 0:E]).then_inc(lg_cp, 1)

                def choose(b):
                    wait(dve, lg_cp, b + 1, apart=True)
                    nc.vector.max(top8, lg).then_inc(t8, 1)
                    wait(dve, t8, b + 1, apart=True)
                    nc.vector.max_index(idx8, top8, lg).then_inc(i8, 1)
                    wait(dve, i8, b + 1)
                    wait(dve, d0, b)
                    nc.vector.tensor_copy(idxf, idx8[:, 0:2]).then_inc(ixf, 1)
                    nc.vector.tensor_tensor(diff, top8[:, 1:2], top8[:, 0:1], ALU.subtract).then_inc(df_done, 1)
                    wait(dve, ixf, b + 1)
                    wait(dve, pos_done, b)
                    nc.vector.tensor_tensor(mask.rearrange("p (k e) -> p k e", k=2),
                                            iota12[:, None, :].broadcast_to([128, 2, E]),
                                            idxf[:, :, None].broadcast_to([128, 2, E]),
                                            ALU.is_equal).then_inc(mk, 1)

                def count(b):
                    wait(dve, pos_done, b + 1)
                    wait(dve, p2, b)
                    nc.vector.tensor_tensor(posm, OT_B[:, 0:2 * E], mask, ALU.mult).then_inc(pm, 1)
                    wait(dve, mac, b + 1)
                    nc.vector.tensor_tensor(macc[:, :], macc[:, :], mask, ALU.add).then_inc(mac, 1)

                def place(b):
                    wait(dve, e10_done, b + 1)
                    nc.vector.tensor_scalar(den, e10, 1.0, None, ALU.add).then_inc(den_done, 1)
                    wait(dve, pm, b + 1)
                    nc.vector.tensor_reduce(pos2, posm.rearrange("p (k e) -> p k e", k=2), AX.X,
                                            ALU.add).then_inc(p2, 1)
                    wait(dve, den_done, b + 1)
                    wait(dve, s_table, 32 * b)
                    nc.vector.reciprocal(entry_t[:, 0, 1:2].bitcast(f32), den).then_inc(w0_done, 1)
                    wait(dve, p2, b + 1)
                    nc.vector.tensor_scalar(over, pos2, float(CAP), float(BIG), ALU.is_ge, ALU.mult).then_inc(ov, 1)
                    wait(dve, w0_done, b + 1)
                    nc.vector.tensor_tensor(entry_t[:, 1, 1:2].bitcast(f32), entry_t[:, 0, 1:2].bitcast(f32), e10,
                                            ALU.mult).then_inc(w1_done, 1)
                    wait(dve, ov, b + 1)
                    nc.vector.tensor_tensor(over, over, pos2, ALU.add).then_inc(ovb, 1)
                    wait(dve, tok_n, b)
                    nc.vector.tensor_copy(entry_t[:, :, 0], tokf.broadcast_to([128, 2])).then_inc(tok_i, 1)
                    wait(dve, ovb, b + 1)
                    nc.vector.scalar_tensor_tensor(out=over[:, 0:1], in0=idxf[:, 0:1], scalar=float(STRIDE),
                                                   in1=over[:, 0:1], op0=ALU.mult, op1=ALU.add)
                    nc.vector.scalar_tensor_tensor(out=over[:, 1:2], in0=idxf[:, 1:2], scalar=float(CP),
                                                   in1=over[:, 1:2], op0=ALU.mult, op1=ALU.add).then_inc(d0, 1)
                    wait(dve, tok_i, b + 1)
                    nc.vector.tensor_scalar(tokf, tokf, 128.0, None, ALU.add).then_inc(tok_n, 1)
                    wait(dve, d0, b + 1)
                    nc.vector.tensor_tensor(dst, over, list_off, ALU.add).then_inc(dst_rdy, 1)

                for l in range(NLOT):
                    if l + 1 < NLOT and LOTS[l + 1][0] == "q":
                        n, part = LOTS[l + 1][1], stage(l + 1)
                        dve.wait_ge(w_mean, n + 1)
                        nc.vector.tensor_tensor(part, part, mean_cols(n)[:, None, :].broadcast_to([128, NC, 128]),
                                                ALU.subtract).then_inc(w_cent, 1)
                    dve.wait_ge(w_hi, l + 1)
                    hi, lo = lot_parts(l)
                    nc.vector.tensor_tensor(lo, stage(l), hi.bitcast(f32), ALU.subtract).then_inc(w_lo, 1)
                    if l == V_IN - 1:
                        split_c(0)
                    if l == Q_IN + 2 * NG - 1:
                        split_x(0)
                        stats_x(0)
                dve.wait_ge(d_small, 48)
                nc.vector.tensor_tensor(wqk, qw_s, kw_s, ALU.mult).then_inc(wqk_done, 1)
                dve.wait_ge(s_const, 1)
                dve.wait_ge(w_lo, NLOT)
                square_k(0)
                square_q(0, 0)
                scale_k(0)
                split_k(0)
                split_q(0, 0)

                def body(b, first=False, last=False):
                    early = isinstance(b, int) and b < 2
                    for g in range(NG):
                        prev = (b, g - 1) if g else (b - 1, NG - 1)
                        nxt = (b, g + 1) if g < NG - 1 else (b + 1, 0)
                        if g == 3 and not first:
                            copy_logits(b - 1)
                        maxima(b, g)
                        if not (first and g == 0):
                            split_o(*prev)
                        if g == 1 and not first:
                            residual(b - 1)
                        if g == 2 and not first:
                            norm2(b - 1)
                        if g == 3 and not early:
                            place(b - 2)
                        if g == 3 and not first:
                            choose(b - 1)
                        normalise(b, g)
                        if g == 3 and not last:
                            split_x(b + 1)
                            square_k(b + 1)
                            stats_x(b + 1)
                            scale_k(b + 1)
                        if not (last and g == NG - 1):
                            square_q(*nxt)
                        if g == 0:
                            split_v(b)
                        if g == 3 and not last:
                            split_k(b + 1)
                        if not (last and g == NG - 1):
                            split_q(*nxt)
                        split_p(b, g)
                        if g == 0 and not last:
                            split_c(b + 1)
                        if g == 1 and not first:
                            stats_2(b - 1)
                        if g == 3 and not first:
                            count(b - 1)

                body(0, first=True)
                body(1)
                with dve.Fori(2, NB - 1) as b:
                    body(b)
                body(NB - 1, last=True)
                place(NB - 2)
                split_o(NB - 1, NG - 1)
                residual(NB - 1)
                stats_2(NB - 1)
                norm2(NB - 1)
                copy_logits(NB - 1)
                choose(NB - 1)
                count(NB - 1)
                place(NB - 1)

            @block.gpsimd
            def _(pool):
                nc.gpsimd.memset(ident[:, :], 0.0)
                nc.gpsimd.memset(ones_b[:, :], 1.0)
                nc.gpsimd.memset(tri[:, :], 1.0)
                nc.gpsimd.iota(iota12[:, :], pattern=[[1, E]], base=0, channel_multiplier=0,
                               allow_small_or_imprecise_dtypes=True)
                nc.gpsimd.iota(tokf, pattern=[[0, 1]], base=0, channel_multiplier=1,
                               allow_small_or_imprecise_dtypes=True)
                nc.gpsimd.memset(sentinel[:, :, 1], 0)
                nc.gpsimd.iota(sentinel[:, :, 0], pattern=[[1, NT]], base=T,
                               channel_multiplier=NT).then_inc(s_zero, 1)
                pool.wait_ge(s_zero, 1)
                nc.gpsimd.affine_select(out=ident[:, :], in_=ident[:, :], compare_op=ALU.not_equal, fill=1.0,
                                        base=0, pattern=[[-1, 128]], channel_multiplier=1)
                nc.gpsimd.affine_select(out=tri[:, :], in_=tri[:, :], compare_op=ALU.is_gt, fill=0.0,
                                        base=0, pattern=[[1, 128]], channel_multiplier=-1).then_inc(s_const, 1)

                def eps_of_x(b):
                    wait(pool, mvx_done, b + 1, apart=True)
                    nc.gpsimd.tensor_scalar(eps_x, mv_x[:, 1:2], HD * ATTN_EPS, HD * ATTN_EPS * LN_EPS,
                                            ALU.mult, ALU.add).then_inc(eps_done, 1)

                def rms_k(b):
                    wait(pool, k_sq, b + 1, apart=True)
                    nc.gpsimd.tensor_scalar(k_ms, k_ssq, 1.0 / HD, ATTN_EPS, ALU.mult, ALU.add).then_inc(k_m, 1)
                    wait(pool, k_m, b + 1)
                    wait(pool, k_sc, b)
                    nc.gpsimd.tensor_tensor(k_rms, k_ms, neghalf, ALU.pow).then_inc(k_r, 1)

                def rms_q(b, g):
                    u = 4 * b + g
                    wait(pool, q_sq, u + 1)
                    if g == 0:
                        wait(pool, eps_done, b + 1)
                    nc.gpsimd.tensor_tensor(q_ms, q_ssq, eps_x.broadcast_to([128, HPG]), ALU.add).then_inc(q_m, 1)
                    wait(pool, q_m, u + 1)
                    wait(pool, exp_done, u)
                    nc.gpsimd.tensor_tensor(q_rms, q_ms, neghalf, ALU.pow).then_inc(q_r, 1)

                def rstd2(b):
                    wait(pool, mv2_done, b + 1, apart=True)
                    nc.gpsimd.tensor_scalar(ve_2, mv_2[:, 1:2], LN_EPS, None, ALU.add).then_inc(ve2_done, 1)
                    wait(pool, ve2_done, b + 1)
                    wait(pool, xn2_done, b)
                    nc.gpsimd.tensor_tensor(rstd_2, ve_2, neghalf[:, 0:1], ALU.pow).then_inc(r2_done, 1)

                def scatter(b):
                    wait_apart(pool, (dst_rdy, b + 1), (w1_done, b + 1))
                    for k in range(2):
                        nc.gpsimd.indirect_dma_start(
                            out=table_d, out_offset=bass.IndirectOffsetOnAxis(ap=dst[:, k:k + 1], axis=0),
                            in_=entry_t[:, k, :], in_offset=None, bounds_check=ROWS - 1,
                            oob_is_err=False).then_inc(s_table, 16)

                pool.wait_ge(mac, 1)
                eps_of_x(0)
                rms_k(0)
                rms_q(0, 0)

                def body(b, first=False, last=False):
                    early = isinstance(b, int) and b < 2
                    for g in range(NG):
                        nxt = (b, g + 1) if g < NG - 1 else (b + 1, 0)
                        if g == 3 and not last:
                            rms_k(b + 1)
                            eps_of_x(b + 1)
                        if not (last and g == NG - 1):
                            rms_q(*nxt)
                        if g == 1 and not first:
                            rstd2(b - 1)
                        if g == 3 and not early:
                            scatter(b - 2)

                body(0, first=True)
                body(1)
                pool.wait_ge(d_sent, 32)
                with pool.Fori(2, NB - 1) as b:
                    body(b)
                body(NB - 1, last=True)
                scatter(NB - 2)
                rstd2(NB - 1)
                scatter(NB - 1)
                pool.wait_ge(s_table, 32 * NB)

        experts(nc, gt=dict(wait=wait, wait_apart=wait_apart, sem=sem, pb=pb, ident=ident, ones_b=ones_b,
                            macc=macc, xn2_d=xn2_d, table_d=table_d), w13=w13, w2T=w2T, out=out)
    return nc


def kernel(x, ctx_2048, L0_xattn_Wq, L0_xattn_Wk, L0_xattn_Wv, L0_xattn_Wo, L0_xattn_q_norm_w,
           L0_xattn_k_norm_w, L0_ffn_gate_w, L0_ffn_w1, L0_ffn_w2, L0_ffn_w3):
    import concourse.bacc as bacc
    from concourse.bass_utils import run_bass_kernel_spmd

    def by_width(a):
        a = np.asarray(a)
        return np.ascontiguousarray(a.reshape(NB, SEQ, NC, 128).transpose(0, 3, 2, 1))

    def pieces(a):
        return np.ascontiguousarray(a.reshape(NC, 128, -1).transpose(1, 0, 2))

    w1, w2, w3 = (np.asarray(a) for a in (L0_ffn_w1, L0_ffn_w2, L0_ffn_w3))
    w13 = np.concatenate([w1, w3], axis=1).transpose(0, 2, 1)
    w13 = np.ascontiguousarray(w13.reshape(E, NC, 128, 2 * F).transpose(0, 2, 1, 3))
    arrays = {
        "x": np.ascontiguousarray(x), "xT": by_width(x), "cT": by_width(ctx_2048),
        "wq": np.ascontiguousarray(L0_xattn_Wq), "wk": np.ascontiguousarray(L0_xattn_Wk),
        "wv": np.ascontiguousarray(L0_xattn_Wv), "wo": np.ascontiguousarray(L0_xattn_Wo),
        "qw": np.asarray(L0_xattn_q_norm_w).reshape(HD, 1), "kw": np.asarray(L0_xattn_k_norm_w).reshape(HD, 1),
        "gateT": pieces(np.asarray(L0_ffn_gate_w).T), "w13": w13,
        "w2T": np.ascontiguousarray(w2.transpose(0, 2, 1)),
    }
    nc = bacc.Bacc("TRN2", target_bir_lowering=False, num_devices=1)
    aps = {n: nc.dram_tensor(n, a.shape, mybir.dt.from_np(a.dtype), kind="ExternalInput").ap()
           for n, a in arrays.items()}
    out = nc.dram_tensor("out", (T + CP, HID), mybir.dt.float32, kind="ExternalOutput").ap()
    build(nc, out=out, **aps)
    result = run_bass_kernel_spmd(nc, [arrays], core_ids=[0])
    return result.results[0]["out"][:T].reshape(NB, SEQ, HID)
```
